# Optimizing a Trainium2 kernel written in Bass

```python
import numpy as np
import jax
import jax.numpy as jnp

def _softmax(x, axis=-1):
    return jax.nn.softmax(x, axis=axis)

def _gelu(x):
    return jax.nn.gelu(x, approximate=True)

def _silu(x):
    return jax.nn.silu(x)

def _sigmoid(x):
    return jax.nn.sigmoid(x)

def _layernorm(x, axis=-1, eps=1e-05):
    m = jnp.mean(x, axis=axis, keepdims=True)
    v = jnp.var(x, axis=axis, keepdims=True)
    return (x - m) / jnp.sqrt(v + eps)

def _scatter_add(tgt, idx, src, axis=0):
    return tgt.at[idx].add(src)

def _segment_sum(src, seg, n):
    return jax.ops.segment_sum(src, seg, n)
kernel_name = 'mk_macaron_d1_jaxref_r8_9bcf20'

def setup_inputs(seed: int=0):
    np.random.seed(seed)
    _w = jnp.asarray

    def _L0_attn_setup():
        import jax, jax.numpy as jnp
        import numpy as np
        B, S, D = (4, 512, 256)
        IDENTITY_WEIGHT = 0.5
        ROT_DIM = D // 2

        def _layernorm(x, gamma, beta, eps=1e-05):
            mu = jnp.mean(x, axis=-1, keepdims=True)
            var = jnp.var(x, axis=-1, keepdims=True)
            return (x - mu) * jax.lax.rsqrt(var + eps) * gamma + beta

        def _rotary(t, rot_dim, theta=10000.0):
            seq = t.shape[-2]
            inv_freq = 1.0 / theta ** (jnp.arange(0, rot_dim, 2, dtype=jnp.float32) / rot_dim)
            freqs = jnp.arange(seq, dtype=jnp.float32)[:, None] * inv_freq[None, :]
            freqs = jnp.repeat(freqs, 2, axis=-1)
            cos, sin = (jnp.cos(freqs), jnp.sin(freqs))
            t_rot, t_pass = (t[..., :rot_dim], t[..., rot_dim:])
            x1, x2 = (t_rot[..., 0::2], t_rot[..., 1::2])
            rot_half = jnp.stack([-x2, x1], axis=-1).reshape(t_rot.shape)
            return jnp.concatenate([t_rot * cos + rot_half * sin, t_pass], axis=-1)

        def _cos_sim(x):
            return x / jnp.linalg.norm(x, axis=-1, keepdims=True)
        key = jax.random.key(seed)
        ks = jax.random.split(key, 3)
        scale = 0.02
        return {'X': jax.random.normal(ks[0], (B, S, D), jnp.float32), 'W_in': jax.random.normal(ks[1], (D, 3 * D), jnp.float32) * scale, 'b_in': jnp.zeros((3 * D,), jnp.float32), 'W_out': jax.random.normal(ks[2], (D, D), jnp.float32) * scale, 'b_out': jnp.zeros((D,), jnp.float32), 'gamma': jnp.ones((D,), jnp.float32), 'beta': jnp.zeros((D,), jnp.float32)}
    _L0_attn_in = _L0_attn_setup()

    def _L0_ffn_setup():
        import jax, jax.numpy as jnp
        import numpy as np
        ALPHA = 1.702
        LIMIT = 7.0
        TOP_K = 4
        B, S, H = (1, 128, 256)
        E, D = (16, 256)
        key = jax.random.key(seed)
        ks = jax.random.split(key, 7)
        s = 0.02
        return {'hidden_states': jax.random.normal(ks[0], (B, S, H), dtype=jnp.float32), 'router_weight': jax.random.normal(ks[1], (E, H), dtype=jnp.float32) * s, 'router_bias': jax.random.normal(ks[2], (E,), dtype=jnp.float32) * s, 'gate_up_proj': jax.random.normal(ks[3], (E, H, 2 * D), dtype=jnp.float32) * s, 'gate_up_proj_bias': jax.random.normal(ks[4], (E, 2 * D), dtype=jnp.float32) * s, 'down_proj': jax.random.normal(ks[5], (E, D, H), dtype=jnp.float32) * s, 'down_proj_bias': jax.random.normal(ks[6], (E, H), dtype=jnp.float32) * s}
    _L0_ffn_in = _L0_ffn_setup()
    _d = {'L0_attn_X': _L0_attn_in['X'], 'L0_attn_W_in': _L0_attn_in['W_in'], 'L0_attn_b_in': _L0_attn_in['b_in'], 'L0_attn_W_out': _L0_attn_in['W_out'], 'L0_attn_b_out': _L0_attn_in['b_out'], 'L0_attn_gamma': _L0_attn_in['gamma'], 'L0_attn_beta': _L0_attn_in['beta'], 'L0_ffn_router_weight': _L0_ffn_in['router_weight'], 'L0_ffn_router_bias': _L0_ffn_in['router_bias'], 'L0_ffn_gate_up_proj': _L0_ffn_in['gate_up_proj'], 'L0_ffn_gate_up_proj_bias': _L0_ffn_in['gate_up_proj_bias'], 'L0_ffn_down_proj': _L0_ffn_in['down_proj'], 'L0_ffn_down_proj_bias': _L0_ffn_in['down_proj_bias']}
    _x0 = _d['L0_attn_X']
    _d['L0_attn_X'] = jax.random.normal(jax.random.fold_in(jax.random.key(seed), 1), (8, 256, 256), dtype=_x0.dtype)
    del _x0
    return _d

def reference(L0_attn_X, L0_attn_W_in, L0_attn_b_in, L0_attn_W_out, L0_attn_b_out, L0_attn_gamma, L0_attn_beta, L0_ffn_router_weight, L0_ffn_router_bias, L0_ffn_gate_up_proj, L0_ffn_gate_up_proj_bias, L0_ffn_down_proj, L0_ffn_down_proj_bias):

    def _L0_attn_ref(X, W_in, b_in, W_out, b_out, gamma, beta):
        import jax, jax.numpy as jnp
        import numpy as np
        B, S, D = (4, 512, 256)
        IDENTITY_WEIGHT = 0.5
        ROT_DIM = D // 2

        def _layernorm(x, gamma, beta, eps=1e-05):
            mu = jnp.mean(x, axis=-1, keepdims=True)
            var = jnp.var(x, axis=-1, keepdims=True)
            return (x - mu) * jax.lax.rsqrt(var + eps) * gamma + beta

        def _rotary(t, rot_dim, theta=10000.0):
            seq = t.shape[-2]
            inv_freq = 1.0 / theta ** (jnp.arange(0, rot_dim, 2, dtype=jnp.float32) / rot_dim)
            freqs = jnp.arange(seq, dtype=jnp.float32)[:, None] * inv_freq[None, :]
            freqs = jnp.repeat(freqs, 2, axis=-1)
            cos, sin = (jnp.cos(freqs), jnp.sin(freqs))
            t_rot, t_pass = (t[..., :rot_dim], t[..., rot_dim:])
            x1, x2 = (t_rot[..., 0::2], t_rot[..., 1::2])
            rot_half = jnp.stack([-x2, x1], axis=-1).reshape(t_rot.shape)
            return jnp.concatenate([t_rot * cos + rot_half * sin, t_pass], axis=-1)

        def _cos_sim(x):
            return x / jnp.linalg.norm(x, axis=-1, keepdims=True)
        Xn = _layernorm(X, gamma, beta)
        QKV = Xn @ W_in + b_in
        Q, K, V = jnp.split(QKV, 3, axis=-1)
        K = _rotary(K, ROT_DIM)
        V = _rotary(V, ROT_DIM)
        A = jnp.sum(_cos_sim(K) * _cos_sim(V), axis=-2)
        A = (1.0 - IDENTITY_WEIGHT) * A + IDENTITY_WEIGHT
        Y = A[:, None, :] * Q
        Y = Y @ W_out + b_out
        return Y + X

    def _L0_ffn_ref(hidden_states, router_weight, router_bias, gate_up_proj, gate_up_proj_bias, down_proj, down_proj_bias):
        import jax, jax.numpy as jnp
        import numpy as np
        ALPHA = 1.702
        LIMIT = 7.0
        TOP_K = 4
        B, S, H = (1, 128, 256)
        E, D = (16, 256)
        batch, seq, hdim = hidden_states.shape
        x = hidden_states.reshape(-1, hdim)
        T = x.shape[0]
        logits = x @ router_weight.T + router_bias
        top_val, top_idx = jax.lax.top_k(logits, TOP_K)
        top_val = jax.nn.softmax(top_val, axis=-1)
        router_scores = jnp.zeros_like(logits).at[jnp.arange(T)[:, None], top_idx].set(top_val)
        gate_up = jnp.einsum('th,ehd->etd', x, gate_up_proj) + gate_up_proj_bias[:, None, :]
        gate = gate_up[..., ::2]
        up = gate_up[..., 1::2]
        gate = jnp.minimum(gate, LIMIT)
        up = jnp.clip(up, -LIMIT, LIMIT)
        glu = gate * jax.nn.sigmoid(gate * ALPHA)
        out = jnp.einsum('etd,edh->eth', (up + 1.0) * glu, down_proj) + down_proj_bias[:, None, :]
        out = out * router_scores.T[:, :, None]
        out = out.sum(axis=0)
        return out.reshape(batch, seq, hdim)
    x = L0_attn_X
    x = x + 0.5 * _L0_ffn_ref(_layernorm(x, axis=-1), L0_ffn_router_weight, L0_ffn_router_bias, L0_ffn_gate_up_proj, L0_ffn_gate_up_proj_bias, L0_ffn_down_proj, L0_ffn_down_proj_bias)
    x = x + _L0_attn_ref(_layernorm(x, axis=-1), L0_attn_W_in, L0_attn_b_in, L0_attn_W_out, L0_attn_b_out, L0_attn_gamma, L0_attn_beta)
    x = x + 0.5 * _L0_ffn_ref(_layernorm(x, axis=-1), L0_ffn_router_weight, L0_ffn_router_bias, L0_ffn_gate_up_proj, L0_ffn_gate_up_proj_bias, L0_ffn_down_proj, L0_ffn_down_proj_bias)
    return x

_drawn_inputs = setup_inputs


def setup_inputs(seed=0):
    import zlib

    import numpy as np

    out = dict(_drawn_inputs(seed))
    spreads = {'L0_attn_b_in': (0.0, 0.8),
     'L0_attn_b_out': (0.0, 0.1),
     'L0_attn_gamma': (1.0, 0.6),
     'L0_attn_beta': (0.0, 2.0)}
    factors = {'L0_ffn_router_weight': 2.804,
     'L0_ffn_router_bias': 26.545,
     'L0_ffn_gate_up_proj_bias': 33.988,
     'L0_ffn_down_proj_bias': 7.484}
    for name, (base, spread) in spreads.items():
        noise = np.random.default_rng([zlib.crc32(name.encode()), seed]).standard_normal(out[name].shape)
        drawn = base * np.exp(spread * noise) if base else spread * noise
        out[name] = jnp.asarray(drawn.astype(out[name].dtype))
    for name, factor in factors.items():
        out[name] = (out[name] * factor).astype(out[name].dtype)
    return out
```

```python
from contextlib import ExitStack

import numpy as np
import concourse.bass as bass
from concourse import mybir

ALU = mybir.AluOpType
ACT = mybir.ActivationFunctionType
F32 = mybir.dt.float32
F16 = mybir.dt.float16
BF16 = mybir.dt.bfloat16
I32 = mybir.dt.int32
U32 = mybir.dt.uint32
AX_X = mybir.AxisListType.X

P = 128
BATCH, SEQ, D = 8, 256, 256
TOKENS = BATCH * SEQ
NT = TOKENS // P
GT = 4
NG = NT // GT
C = D // P
EXPERTS, TOP_K = 16, 4
HID = 256
GU = 2 * HID
UNROLL = 4
TILES = TOKENS * TOP_K // P + EXPERTS - 1
TILES = -(-TILES // UNROLL) * UNROLL
ROT = D // 2
HALF = ROT // 2
LIMIT, ALPHA = 7.0, 1.702
EPS = 1e-5
BROW = GU + D
BCOL = EXPERTS * BROW // P

CONST = {}
for _n, _w in (("ident", P), ("lowm", P), ("iota", P), ("seg", EXPERTS * NT), ("tid1", NT), ("part128", 1),
               ("spare1", TILES), ("cos", 2 * ROT), ("sin", 2 * ROT)):
    CONST[_n] = (sum(w for _, w in CONST.values()), _w)
CONST_W = sum(w for _, w in CONST.values())
ROWS = {"rbias": (0, EXPERTS), "bkv": (EXPERTS, 2 * D), "bout": (EXPERTS + 2 * D, D)}
ROWS_W = EXPERTS + 3 * D
PW = {"rw": (0, C * EXPERTS), "gamma": (C * EXPERTS, C), "beta": (C * EXPERTS + C, C), "bq": (C * EXPERTS + 2 * C, C)}
PW_W = C * EXPERTS + 3 * C


def macaron_kernel(nc, x, consts, rows, pweights, w_in, w_out, w_gu, w_down, bias, out):
    x_v = x.rearrange("(i p) d -> p i d", p=P)
    out_v = out.rearrange("(i p) d -> p i d", p=P)
    xn_dram = nc.dram_tensor("xn_dram", [TOKENS, D], F32, kind="Internal").ap()
    y_dram = nc.dram_tensor("y_dram", [TOP_K * TOKENS + TILES * P, D], F32, kind="Internal").ap()
    y_v = y_dram[0:TOP_K * TOKENS, :].rearrange("(k i p) d -> p k i d", k=TOP_K, p=P)
    bias_dram = nc.dram_tensor("bias_dram", [3, EXPERTS * BROW], BF16, kind="Internal").ap()
    xn_v = xn_dram.rearrange("(i p) d -> p i d", p=P)

    with ExitStack() as ctx:
        def sb(name, shape, dt=F32):
            return ctx.enter_context(nc.sbuf_tensor(name, shape, dt))

        def sem(name):
            return ctx.enter_context(nc.semaphore(name))

        bank = [ctx.enter_context(nc.psum_tensor(f"bank{n}", [P, 512], F32)) for n in range(8)]

        wgu = sb("wgu", [P, EXPERTS, C, GU])
        wdn = sb("wdn", [P, EXPERTS, C, D])
        brow = sb("brow", [P, EXPERTS, BROW], BF16)
        X = sb("X", [P, NT, D])
        xnT = sb("xnT", [P, C, TOKENS])
        win = sb("win", [P, C, 3 * D])
        wout = sb("wout", [P, C, D])
        cst = sb("cst", [P, CONST_W])
        rowv = sb("rowv", [P, ROWS_W])
        pw = sb("pw", [P, PW_W])
        xn = sb("xn", [P, 2, GT, D])
        onesf = sb("onesf", [P, P])
        onesb = sb("onesb", [P, P], BF16)
        iota16 = sb("iota16", [P, P], F16)
        epsc = sb("epsc", [P, 1])
        stats = sb("stats", [P, 2, GT, 6])
        mv = sb("mv", [P, 2, GT, 2])
        rstd = sb("rstd", [P, 2, GT])
        tops = sb("tops", [P, NT, 8])
        wk = sb("wk", [P, NT, TOP_K])
        gidx = sb("gidx", [P, TILES], U32)
        sidx = sb("sidx", [P, TILES], U32)
        etile = sb("etile", [1, P], I32)
        gcol = sb("gcol", [P, UNROLL], U32)
        scol = sb("scol", [P, UNROLL], U32)
        WORK = 24 * 256
        work = sb("work", [P, WORK])

        def wk_area(at, *shape):
            n = int(np.prod(shape))
            names = "abc"[:len(shape)]
            v = work[:, at:at + n]
            if len(shape) == 1:
                return v
            return v.rearrange(f"p ({' '.join(names)}) -> p {' '.join(names)}",
                               **{names[i]: shape[i] for i in range(len(shape))})

        xg = wk_area(0, 4, D)
        yb = wk_area(4 * D, 4, D)
        xT = wk_area(8 * D, 2, D)
        hT = wk_area(10 * D, 2, D)
        gate = wk_area(12 * D, 2, D)
        up = wk_area(14 * D, 2, D)
        prod = wk_area(16 * D, 2, D)
        sig = wk_area(18 * D, 2, D)
        hid = wk_area(20 * D, 2, D)
        yc = wk_area(0, 2, TOP_K, D)
        logits = wk_area(0, NT, EXPERTS)
        topif = wk_area(256, NT, TOP_K)
        topi = wk_area(320, NT, 8).bitcast(U32)
        hot = wk_area(512, TOP_K, EXPERTS, NT)
        hot2 = wk_area(1536, 2, EXPERTS * NT)
        mask = wk_area(2048, EXPERTS * NT)
        pre = wk_area(2304, EXPERTS * NT)
        posall = wk_area(2560, EXPERTS, NT)
        hotpos = wk_area(2816, TOP_K, EXPERTS, NT)
        pos = wk_area(3840, TOP_K * NT)
        jf = wk_area(3904, TOP_K * NT)
        sf = wk_area(3968, TOP_K * NT)
        posi = wk_area(4032, TOP_K * NT).bitcast(I32)
        ji = wk_area(4096, TOP_K * NT).bitcast(I32)
        cnti = wk_area(4160, EXPERTS).bitcast(I32)
        nt128 = wk_area(4176, EXPERTS).bitcast(I32)
        tend = wk_area(4192, EXPERTS)
        base = wk_area(4208, EXPERTS)
        ecmp = wk_area(4224, EXPERTS)
        ecol = wk_area(4240, 1)
        wsum = wk_area(448, NT)
        wrec = wk_area(464, NT)
        codes = wk_area(4244, TOP_K, TILES)
        csum = wk_area(4564, TILES)
        ksum = wk_area(4644, TILES)
        ppres = wk_area(4724, TILES)
        RING = 8
        slot_hot = wk_area(4804, RING * P // 2).bitcast(F16).rearrange("p (r s) -> p r s", r=RING)
        tile_hot = wk_area(4804 + RING * P // 2, RING * TILES // 2).bitcast(F16).rearrange("p (r s) -> p r s", r=RING)
        kv = wk_area(2048, 2, 2 * D)
        rot = wk_area(3072, 2, ROT)
        rots = wk_area(3328, 2, ROT)
        rotd = wk_area(3584, 2, ROT)
        kvprod = wk_area(3840, GT, D)
        aw = wk_area(4864, 2, C, D)
        qT = sb("qT", [P, C, GT * P])
        junk = wk_area(4864 + 2 * C * D, D)
        ssq = sb("ssq", [P, GT, 2])
        nrm = sb("nrm", [P, GT, 2])
        rkv = sb("rkv", [P, GT])
        amix = sb("amix", [P, 2, C])
        BIAS_AT = WORK - 5 * BCOL
        bsrc = wk_area(BIAS_AT, BCOL)
        bres = wk_area(BIAS_AT + BCOL, BCOL)
        bres2 = wk_area(BIAS_AT + 2 * BCOL, BCOL)
        bpart = wk_area(BIAS_AT + 3 * BCOL, 3 * BCOL // 2).bitcast(BF16).rearrange("p (n j) -> p n j", n=3)

        def const(name):
            at, w = CONST[name]
            return cst[:, at:at + w]

        def row(name):
            at, w = ROWS[name]
            return rowv[:, at:at + w]

        def pwt(name):
            at, w = PW[name]
            return pw[:, at:at + w]

        rw = pwt("rw").rearrange("p (c e) -> p c e", c=C)

        const_in, rows_in, pw_in, bias_in, attw_in, w_loaded = map(
            sem, ("const_in", "rows_in", "pw_in", "bias_in", "attw_in", "w_loaded"))
        x_in = [sem(f"x_in{g}") for g in range(NG)]
        bias_split, bias_stored, bias_rows, bias_zero, ones_set, iota_set = map(
            sem, ("bias_split", "bias_stored", "bias_rows", "bias_zero", "ones_set", "iota_set"))
        dve_step = sem("dve_step")
        out_stored = sem("out_stored")

        def signals(tag, names, **lists):
            one = {n: sem(f"{tag}_{n}") for n in names.split()}
            one.update({n: [sem(f"{tag}_{n}{m}") for m in range(count)] for n, count in lists.items()})
            return one

        FFN = ("var std xn xn_ps xnT logit_ps logit wexp_in wexp pre cnt_ps hot slot_hot tile_hot place_ps cols gcol scol ecol etile_ps "
               "etile gidx sidx xt_ps xt gu_ps gate gu_used prod sig hid ht_ps ht y_ps y")
        ffn = [signals(f"ffn{f}", FFN + " combined", xn_stored=2, gathered=UNROLL, scattered=UNROLL, y_back=2)
               for f in range(2)]
        att = signals("att", "var std xn xn_ps xnT kv_ps kv sq ssq norm ssin kvprod rkv a_ps amix aw q_ps qT o_ps x x2 sum")

        block = ctx.enter_context(nc.Block())

        @block.sync
        def _(sp):
            sp.dma_start(cst[:, :], consts).then_inc(const_in, 16)
            for g in range(NG):
                sp.dma_start(X[:, g * GT:(g + 1) * GT, :], x_v[:, g * GT:(g + 1) * GT, :]).then_inc(x_in[g], 16)
            sp.dma_start(pw[:, :], pweights).then_inc(pw_in, 16)
            sp.dma_start(rowv[:, :], rows.partition_broadcast(P)).then_inc(rows_in, 16)
            sp.dma_start(bsrc, bias).then_inc(bias_in, 16)
            for e in range(EXPERTS):
                sp.dma_start(wgu[:, e], w_gu[:, e]).then_inc(w_loaded, 16)
                sp.dma_start(wdn[:, e], w_down[:, e]).then_inc(w_loaded, 16)
            sp.dma_start(win[:, :, :], w_in).then_inc(attw_in, 16)
            sp.dma_start(wout[:, :, :], w_out).then_inc(attw_in, 16)
            for f in range(2):
                for u in range(UNROLL):
                    sp.wait_ge(ffn[f]["scattered"][u], 16 * TILES // UNROLL)
                for i in range(NT):
                    if i >= 2:
                        sp.wait_ge(ffn[f]["combined"], i - 1)
                    sp.dma_start(yc[:, i % 2], y_v[:, :, i, :]).then_inc(ffn[f]["y_back"][i % 2], 16)
            for i in range(NT):
                sp.wait_ge(ffn[1]["combined"], i + 1)
                sp.dma_start(out_v[:, i, :], X[:, i, :]).then_inc(out_stored, 16)
            sp.wait_ge(out_stored, 16 * NT)

        @block.gpsimd
        def _(pool):
            nc.gpsimd.memset(onesf[:, :], 1.0).then_inc(ones_set, 1)
            nc.gpsimd.memset(onesb[:, :], 1.0).then_inc(ones_set, 1)
            nc.gpsimd.memset(epsc[:, :], EPS).then_inc(ones_set, 1)
            nc.gpsimd.memset(brow[:, :, :], 0.0).then_inc(bias_zero, 1)

            def tile_hots(s):
                pool.wait_ge(iota_set, 1)
                pool.wait_ge(s["hot"], 1)
                for n in range(TOP_K * NT):
                    if n >= RING:
                        pool.wait_ge(s["place_ps"], n - RING + 1)
                    nc.gpsimd.tensor_scalar(tile_hot[:, n % RING, :], const("iota")[:, 0:TILES], jf[:, n:n + 1],
                                            const("tid1")[:, n % NT:n % NT + 1], ALU.is_equal,
                                            ALU.mult).then_inc(s["tile_hot"], 1)

            def tile(s, j, j0, u, more=True):
                if more:
                    pool.wait_ge(s["xt_ps"], j + 1)
                    gather(s, j + UNROLL, u)
                scatter(s, j, j0, u)

            def copy_cols(s, dst, src, signal, count):
                nc.gpsimd.tensor_copy(dst, src).then_inc(signal, 1)
                pool.wait_ge(signal, count)
                pool.sem_inc(s["cols"], 1)

            def gather(s, j, u):
                copy_cols(s, gcol[:, u:u + 1], gidx[:, bass.ds(j, 1)], s["gcol"], j + 1)
                nc.gpsimd.indirect_dma_start(
                    out=xg[:, u, :], out_offset=None, in_=xn_dram,
                    in_offset=bass.IndirectOffsetOnAxis(ap=gcol[:, u:u + 1], axis=0)).then_inc(s["gathered"][u], 16)

            def scatter(s, j, j0, u):
                if j0 is not None:
                    pool.wait_ge(s["scattered"][u], 4 * j0)
                pool.wait_ge(s["y"], j + 1)
                copy_cols(s, scol[:, u:u + 1], sidx[:, bass.ds(j, 1)], s["scol"], j + 1)
                nc.gpsimd.indirect_dma_start(
                    out=y_dram, out_offset=bass.IndirectOffsetOnAxis(ap=scol[:, u:u + 1], axis=0),
                    in_=yb[:, u, :], in_offset=None).then_inc(s["scattered"][u], 16)

            pool.wait_ge(bias_split, 1)
            nc.gpsimd.dma_start(bias_dram.rearrange("n (p j) -> p n j", p=P), bpart).then_inc(bias_stored, 16)
            pool.wait_ge(bias_stored, 16)
            pool.wait_ge(bias_zero, 1)
            nc.gpsimd.dma_start(brow[0:3, :, :].rearrange("n e j -> n (e j)"), bias_dram).then_inc(bias_rows, 16)
            for f in range(2):
                s = ffn[f]
                tile_hots(s)
                pool.wait_ge(s["gidx"], 1)
                pool.wait_ge(s["sidx"], 1)
                for b in range(2):
                    pool.wait_ge(s["xn_stored"][b], 16 * NG // 2)
                for u in range(UNROLL):
                    gather(s, u, u)
                for u in range(UNROLL):
                    tile(s, u, None, u)
                with pool.Fori(UNROLL, TILES - 2 * UNROLL + 1, UNROLL) as j0:
                    for u in range(UNROLL):
                        tile(s, j0 + u, j0, u)
                for u in range(UNROLL):
                    tile(s, TILES - UNROLL + u, TILES - UNROLL, u, more=False)

        @block.scalar
        def _(act):
            act.wait_ge(ones_set, 3)

            def std_of(s, g):
                act.wait_ge(s["var"], g + 1)
                nc.scalar.activation(rstd[:, g % 2, :], mv[:, g % 2, :, 1], ACT.Sqrt,
                                     bias=epsc[:, 0:1]).then_inc(s["std"], 1)

            def take_xnT(s, g, affine):
                for c in range(C):
                    act.wait_ge(s["xn_ps"], C * g + c + 1)
                    dst = xnT[:, c, g * GT * P:(g + 1) * GT * P]
                    src = bank[C * (g % 2) + c][:, :]
                    if affine:
                        nc.scalar.activation(dst, src, ACT.Identity, bias=pwt("beta")[:, c:c + 1],
                                             scale=pwt("gamma")[:, c:c + 1]).then_inc(s["xnT"], 1)
                    else:
                        nc.scalar.activation(dst, src, ACT.Copy).then_inc(s["xnT"], 1)

            def ffn_front(s, f):
                std_of(s, 0)
                for g in range(NG):
                    if g + 1 < NG:
                        std_of(s, g + 1)
                    act.wait_ge(s["xn"], g + 1)
                    nc.scalar.dma_start(xn_v[:, g * GT:(g + 1) * GT, :], xn[:, g % 2]).then_inc(s["xn_stored"][g % 2], 16)
                    take_xnT(s, g, False)
                act.wait_ge(s["wexp_in"], 1)
                nc.scalar.activation(wk[:, :, :], wk[:, :, :], ACT.Exp).then_inc(s["wexp"], 1)

            def tile(s, j, j0, u, nxt, prv, prv2, lo):
                b = u % 2
                if nxt:
                    take_xt(s, j + 1, (u + 1) % 2, lo + 1)
                act.wait_ge(s["gate"], j + 1)
                if lo >= 2:
                    act.wait_ge(s["hid"], j - 1)
                nc.scalar.activation(sig[:, b], gate[:, b], ACT.Sigmoid, scale=ALPHA).then_inc(s["sig"], 1)
                if prv:
                    take_ht(s, j - 1, (u + 1) % 2, lo - 1)
                if prv2:
                    take_y(s, j - 2, (u + 2) % 4, lo - 2)

            def take_xt(s, j, b, lo):
                act.wait_ge(s["xt_ps"], j + 1)
                if lo >= 2:
                    act.wait_ge(s["gu_ps"], j - 1)
                nc.scalar.activation(xT[:, b], bank[b][:, 0:D], ACT.Copy).then_inc(s["xt"], 1)

            def take_ht(s, j, b, lo):
                act.wait_ge(s["ht_ps"], j + 1)
                if lo >= 2:
                    act.wait_ge(s["y_ps"], j - 1)
                nc.scalar.activation(hT[:, b], bank[4 + b][:, 0:D], ACT.Copy).then_inc(s["ht"], 1)

            def take_y(s, j, u, lo):
                act.wait_ge(s["y_ps"], j + 1)
                if lo >= 4:
                    act.wait_ge(s["scattered"][u], 4 * j - 4 * u)
                nc.scalar.activation(yb[:, u], bank[6 + u % 2][:, 0:D], ACT.Copy).then_inc(s["y"], 1)

            def tile_loop(s):
                take_xt(s, 0, 0, 0)
                for u in range(2 * UNROLL):
                    tile(s, u, None, u % UNROLL, True, u >= 1, u >= 2, u)
                with act.Fori(2 * UNROLL, TILES - 2 * UNROLL + 1, UNROLL) as j0:
                    for u in range(UNROLL):
                        tile(s, j0 + u, j0, u, True, True, True, 8)
                for u in range(UNROLL):
                    j = TILES - UNROLL + u
                    tile(s, j, None, u, u < UNROLL - 1, True, True, j)
                take_ht(s, TILES - 1, 1, TILES - 1)
                take_y(s, TILES - 2, 2, TILES - 2)
                take_y(s, TILES - 1, 3, TILES - 1)

            def attention(s):
                for g in range(NG):
                    act.wait_ge(s["var"], 2 * g + 1)
                    nc.scalar.activation(rstd[:, 0, :], mv[:, 0, :, 1], ACT.Sqrt, bias=epsc[:, 0:1]).then_inc(s["std"], 1)
                    act.wait_ge(s["var"], 2 * g + 2)
                    nc.scalar.activation(rstd[:, 1, :], mv[:, 1, :, 1], ACT.Sqrt, bias=epsc[:, 0:1]).then_inc(s["std"], 1)
                    act.wait_ge(pw_in, 16)
                    for c in range(C):
                        act.wait_ge(s["xn_ps"], C * g + c + 1)
                        nc.scalar.activation(xnT[:, c, g * GT * P:(g + 1) * GT * P], bank[c][:, :], ACT.Identity,
                                             bias=pwt("beta")[:, c:c + 1],
                                             scale=pwt("gamma")[:, c:c + 1]).then_inc(s["xnT"], 1)
                    for t in range(GT):
                        n = g * GT + t
                        act.wait_ge(s["kv"], n + 1)
                        if t == 0 and g >= 1:
                            act.wait_ge(s["norm"], g)
                        for m in range(2):
                            if n or m:
                                act.wait_ge(s["ssq"], 2 * n + m)
                            nc.scalar.activation(junk[:, :], kv[:, t % 2, m * D:(m + 1) * D], ACT.Square,
                                                 accum_out=ssq[:, t, m:m + 1]).then_inc(s["ssq"], 1)
                    act.wait_ge(s["ssq"], 2 * GT * (g + 1))
                    if g >= 1:
                        act.wait_ge(s["rkv"], g)
                    nc.scalar.activation(nrm[:, :, :], ssq[:, :, :], ACT.Sqrt).then_inc(s["norm"], 1)
                    for c in range(C):
                        act.wait_ge(s["q_ps"], C * g + c + 1)
                        if g >= 1:
                            act.wait_ge(s["o_ps"], GT * g)
                        nc.scalar.activation(qT[:, c, :], bank[5 + c][:, :], ACT.Identity,
                                             bias=pwt("bq")[:, c:c + 1]).then_inc(s["qT"], 1)

            ffn_front(ffn[0], 0)
            tile_loop(ffn[0])
            attention(att)
            ffn_front(ffn[1], 1)
            tile_loop(ffn[1])

        @block.tensor
        def _(pe):
            ident = const("ident")

            def group_transposes(s, g, b, xb):
                for c in range(C):
                    for t in range(GT):
                        mm = nc.tensor.transpose(bank[b + c][:, t * P:(t + 1) * P],
                                                 xn[:, xb, t, c * P:(c + 1) * P], ident)
                    mm.then_inc(s["xn_ps"], 1)

            def ffn_front(s):
                for g in range(NG):
                    pe.wait_ge(s["xn"], g + 1)
                    if g >= 2:
                        pe.wait_ge(s["xnT"], C * (g - 1))
                    group_transposes(s, g, C * (g % 2), g % 2)
                    pe.wait_ge(s["xnT"], C * (g + 1))
                    if g >= 2:
                        pe.wait_ge(s["logit"], g - 1)
                    for t in range(GT):
                        for c in range(C):
                            mm = nc.tensor.matmul(bank[4 + g % 2][:, t * EXPERTS:(t + 1) * EXPERTS],
                                                  xnT[:, c, (g * GT + t) * P:(g * GT + t + 1) * P], rw[:, c, :],
                                                  start=(c == 0), stop=(c == C - 1))
                    mm.then_inc(s["logit_ps"], 1)

            def routing(s):
                pe.wait_ge(s["pre"], 1)
                nc.tensor.matmul(bank[6][:, 0:EXPERTS * NT], onesf[:, :], pre, start=True, stop=False)
                nc.tensor.matmul(bank[6][:, 0:EXPERTS * NT], const("lowm"), mask, start=False, stop=True)
                nc.tensor.matmul(bank[6][:, EXPERTS * NT:EXPERTS * NT + EXPERTS], onesf[:, :],
                                 pre.rearrange("p (e i) -> p e i", e=EXPERTS)[:, :, NT - 1],
                                 start=True, stop=True).then_inc(s["cnt_ps"], 1)
                pe.wait_ge(s["ecol"], 1)
                nc.tensor.matmul(bank[6][0:1, 0:P], ecol, ident, start=True, stop=True).then_inc(s["etile_ps"], 1)
                for n in range(TOP_K * NT):
                    pe.wait_ge(s["slot_hot"], n + 1)
                    pe.wait_ge(s["tile_hot"], n + 1)
                    k, i = divmod(n, NT)
                    nc.tensor.matmul(bank[7][:, k * TILES:(k + 1) * TILES], slot_hot[:, n % RING, :],
                                     tile_hot[:, n % RING, :], start=(i == 0),
                                     stop=(i == NT - 1)).then_inc(s["place_ps"], 1)

            def turn_x(s, j, u, lo):
                pe.wait_ge(s["gathered"][u], 4 * j - 4 * u + 16)
                if lo >= 2:
                    pe.wait_ge(s["xt"], j - 1)
                for c in range(C):
                    mm = nc.tensor.transpose(bank[u % 2][:, c * P:(c + 1) * P], xg[:, u, c * P:(c + 1) * P], ident)
                mm.then_inc(s["xt_ps"], 1)

            def gate_up(s, j, b, lo):
                e = pe.value_load(etile[0:1, bass.ds(j, 1)], min_val=0, max_val=EXPERTS - 1)
                pe.wait_ge(s["xt"], j + 1)
                if lo >= 2:
                    pe.wait_ge(s["gu_used"], j - 1)
                acc = bank[2 + b][:, :]
                nc.tensor.matmul(acc, onesb[:, :], brow[:, bass.ds(e, 1), 0:GU].rearrange("p o n -> p (o n)"),
                                 start=True, stop=False)
                for c in range(C):
                    mm = nc.tensor.matmul(acc, xT[:, b, c * P:(c + 1) * P],
                                          wgu[:, bass.ds(e, 1), c, :].rearrange("p o n -> p (o n)"),
                                          start=False, stop=(c == C - 1))
                mm.then_inc(s["gu_ps"], 1)

            def turn_h(s, j, b, lo):
                pe.wait_ge(s["hid"], j + 1)
                if lo >= 2:
                    pe.wait_ge(s["ht"], j - 1)
                for c in range(C):
                    mm = nc.tensor.transpose(bank[4 + b][:, c * P:(c + 1) * P], hid[:, b, c * P:(c + 1) * P], ident)
                mm.then_inc(s["ht_ps"], 1)

            def down(s, j, b, lo):
                e = pe.value_load(etile[0:1, bass.ds(j, 1)], min_val=0, max_val=EXPERTS - 1)
                pe.wait_ge(s["ht"], j + 1)
                if lo >= 2:
                    pe.wait_ge(s["y"], j - 1)
                acc = bank[6 + b][:, 0:D]
                nc.tensor.matmul(acc, onesb[:, :], brow[:, bass.ds(e, 1), GU:BROW].rearrange("p o n -> p (o n)"),
                                 start=True, stop=False)
                for c in range(C):
                    mm = nc.tensor.matmul(acc, hT[:, b, c * P:(c + 1) * P],
                                          wdn[:, bass.ds(e, 1), c, :].rearrange("p o n -> p (o n)"),
                                          start=False, stop=(c == C - 1))
                mm.then_inc(s["y_ps"], 1)

            def tile(s, j, u, nxt, prv, prv2, lo):
                if nxt:
                    turn_x(s, j + 1, (u + 1) % UNROLL, lo + 1)
                gate_up(s, j, u % 2, lo)
                if prv:
                    turn_h(s, j - 1, (u + 1) % 2, lo - 1)
                if prv2:
                    down(s, j - 2, u % 2, lo - 2)

            def tile_loop(s, first):
                pe.wait_ge(s["etile"], 1)
                if first:
                    pe.wait_ge(w_loaded, 32 * EXPERTS)
                    pe.wait_ge(bias_rows, 16)
                turn_x(s, 0, 0, 0)
                for u in range(UNROLL):
                    tile(s, u, u, True, u >= 1, u >= 2, u)
                with pe.Fori(UNROLL, TILES - 2 * UNROLL + 1, UNROLL) as j0:
                    for u in range(UNROLL):
                        tile(s, j0 + u, u, True, True, True, 8)
                for u in range(UNROLL):
                    j = TILES - UNROLL + u
                    tile(s, j, u, u < UNROLL - 1, True, True, j)
                turn_h(s, TILES - 1, 1, TILES - 1)
                down(s, TILES - 2, 0, TILES - 2)
                down(s, TILES - 1, 1, TILES - 1)

            def attention(s):
                for g in range(NG):
                    pe.wait_ge(s["xn"], g + 1)
                    if g >= 1:
                        pe.wait_ge(s["xnT"], C * g)
                    group_transposes(s, g, 0, 1)
                    pe.wait_ge(s["xnT"], C * (g + 1))
                    for t in range(GT):
                        n = g * GT + t
                        if n >= 2:
                            pe.wait_ge(s["kv"], n - 1)
                        for c in range(C):
                            mm = nc.tensor.matmul(bank[2 + n % 2][:, :], xnT[:, c, n * P:(n + 1) * P],
                                                  win[:, c, D:3 * D], start=(c == 0), stop=(c == C - 1))
                        mm.then_inc(s["kv_ps"], 1)
                    for m in range(C):
                        if g >= 1:
                            pe.wait_ge(s["qT"], C * (g - 1) + m + 1)
                        for c in range(C):
                            mm = nc.tensor.matmul(bank[5 + m][:, :], win[:, c, m * P:(m + 1) * P],
                                                  xnT[:, c, g * GT * P:(g + 1) * GT * P],
                                                  start=(c == 0), stop=(c == C - 1))
                        mm.then_inc(s["q_ps"], 1)
                    pe.wait_ge(s["rkv"], g + 1)
                    pe.wait_ge(s["kvprod"], GT * (g + 1))
                    if g >= 1:
                        pe.wait_ge(s["amix"], g)
                    for b in range(2):
                        for c in range(C):
                            for h in range(2):
                                t = 2 * b + h
                                mm = nc.tensor.matmul(bank[4][:, 2 * b + c:2 * b + c + 1],
                                                      kvprod[:, t, c * P:(c + 1) * P], rkv[:, t:t + 1],
                                                      start=(h == 0), stop=(h == 1))
                    mm.then_inc(s["a_ps"], 1)
                    for t in range(GT):
                        n = g * GT + t
                        if t % 2 == 0:
                            pe.wait_ge(s["aw"], 2 * g + t // 2 + 1)
                        if t == 0:
                            pe.wait_ge(s["qT"], C * (g + 1))
                        if n >= 1:
                            pe.wait_ge(s["x2"], n)
                        for c in range(C):
                            mm = nc.tensor.matmul(bank[7][:, 0:D], qT[:, c, t * P:(t + 1) * P], aw[:, t // 2, c, :],
                                                  start=(c == 0), stop=(c == C - 1))
                        mm.then_inc(s["o_ps"], 1)

            pe.wait_ge(const_in, 16)
            pe.wait_ge(pw_in, 16)
            ffn_front(ffn[0])
            pe.wait_ge(ones_set, 3)
            routing(ffn[0])
            tile_loop(ffn[0], True)
            pe.wait_ge(attw_in, 32)
            attention(att)
            ffn_front(ffn[1])
            routing(ffn[1])
            tile_loop(ffn[1], False)

        @block.vector
        def _(dve):
            done = [0]
            V = nc.vector

            def step(ins):
                done[0] += 1
                ins.then_inc(dve_step, 1)
                return done[0]

            def settled(n=None):
                dve.wait_ge(dve_step, done[0] if n is None else n)

            def tile_stats(s, g, b, src):
                for t in range(GT):
                    step(V.bn_stats(stats[:, b, t, :], src(g * GT + t)))
                settled()
                for t in range(GT):
                    m = V.bn_aggr(mv[:, b, t, :], stats[:, b, t, :])
                    if t < GT - 1:
                        step(m)
                    else:
                        m.then_inc(s["var"], 1)

            def normalise(s, b, count, g, src, dst, signal=None):
                dve.wait_ge(s["std"], count)
                step(V.reciprocal(rstd[:, b, :], rstd[:, b, :]))
                dve.wait_ge(s["var"], count)
                settled()
                for t in range(GT):
                    m = V.tensor_scalar(dst(t), src(g * GT + t), mv[:, b, t, 0:1], rstd[:, b, t:t + 1],
                                        ALU.subtract, ALU.mult)
                    if t == GT - 1 and signal is not None:
                        m.then_inc(signal, 1)
                    else:
                        step(m)

            def top4(s, g):
                dve.wait_ge(s["logit_ps"], g + 1)
                V.tensor_tensor(logits[:, g * GT:(g + 1) * GT, :],
                                bank[4 + g % 2][:, 0:GT * EXPERTS].rearrange("p (t e) -> p t e", e=EXPERTS),
                                row("rbias").unsqueeze(1).to_broadcast([P, GT, EXPERTS]),
                                ALU.add).then_inc(s["logit"], 1)
                dve.wait_ge(s["logit"], g + 1)
                for t in range(g * GT, (g + 1) * GT):
                    step(V.max(tops[:, t, :], logits[:, t, :]))
                settled()
                for t in range(g * GT, (g + 1) * GT):
                    step(V.max_index(topi[:, t, :], tops[:, t, :], logits[:, t, :]))

            def ffn_front(s, f):
                def stats_of(g):
                    if f == 0:
                        dve.wait_ge(x_in[g], 16)
                    tile_stats(s, g, g % 2, lambda n: X[:, n, :])

                stats_of(0)
                for g in range(NG):
                    if g + 1 < NG:
                        stats_of(g + 1)
                    if g >= 2:
                        dve.wait_ge(s["xn_stored"][g % 2], 16 * (g // 2))
                        dve.wait_ge(s["xn_ps"], C * (g - 1))
                    normalise(s, g % 2, g + 1, g, lambda n: X[:, n, :], lambda t: xn[:, g % 2, t, :], s["xn"])
                    if g >= 1:
                        top4(s, g - 1)
                top4(s, NG - 1)

            def routing(s):
                settled()
                step(V.tensor_copy(topif[:, :, :], topi[:, :, 0:TOP_K]))
                V.tensor_tensor(wk[:, :, :], tops[:, :, 0:TOP_K],
                                tops[:, :, 0:1].to_broadcast([P, NT, TOP_K]), ALU.subtract).then_inc(s["wexp_in"], 1)
                settled()
                step(V.tensor_tensor(hot[:, :, :, :],
                                     const("iota")[:, 0:EXPERTS].unsqueeze(1).unsqueeze(3)
                                     .to_broadcast([P, TOP_K, EXPERTS, NT]),
                                     topif.rearrange("p i k -> p k i").unsqueeze(2)
                                     .to_broadcast([P, TOP_K, EXPERTS, NT]), ALU.is_equal))
                settled()
                flat = hot.rearrange("p k e i -> p k (e i)")
                step(V.tensor_tensor(hot2, flat[:, 0:2, :], flat[:, 2:4, :], ALU.add))
                settled()
                step(V.tensor_tensor(mask, hot2[:, 0, :], hot2[:, 1, :], ALU.add))
                settled()
                V.tensor_tensor_scan(pre, const("seg"), mask, 0.0, ALU.mult, ALU.add).then_inc(s["pre"], 1)
                dve.wait_ge(s["wexp"], 1)
                step(V.tensor_reduce(wsum, wk[:, :, :], AX_X, ALU.add))
                settled()
                step(V.reciprocal(wrec, wsum))
                settled()
                step(V.scalar_tensor_tensor(wk[:, :, :], wk[:, :, :], 0.5,
                                            wrec.unsqueeze(2).to_broadcast([P, NT, TOP_K]), ALU.mult, ALU.mult))
                dve.wait_ge(s["cnt_ps"], 1)
                step(V.tensor_scalar(cnti, bank[6][:, EXPERTS * NT:EXPERTS * NT + EXPERTS], float(P - 1), None, ALU.add))
                settled()
                step(V.tensor_scalar(nt128, cnti, 7, 7, ALU.logical_shift_right, ALU.logical_shift_left))
                settled()
                step(V.tensor_tensor_scan(tend, onesf[:, 0:EXPERTS], nt128, 0.0, ALU.mult, ALU.add))
                settled()
                step(V.tensor_tensor(base, tend, nt128, ALU.subtract))
                settled()
                step(V.tensor_tensor(posall[:, :, :],
                                     bank[6][:, 0:EXPERTS * NT].rearrange("p (e i) -> p e i", e=EXPERTS),
                                     base.unsqueeze(2).to_broadcast([P, EXPERTS, NT]), ALU.add))
                settled()
                step(V.tensor_tensor(hotpos.rearrange("p k e i -> p k (e i)"), flat,
                                     posall.rearrange("p e i -> p (e i)").unsqueeze(1)
                                     .to_broadcast([P, TOP_K, EXPERTS * NT]), ALU.mult))
                step(V.tensor_scalar(ecmp, tend, const("part128"), None, ALU.is_le))
                settled()
                step(V.tensor_reduce(pos.rearrange("p (k i) -> p k i", k=TOP_K),
                                     hotpos.rearrange("p k e i -> p k i e"), AX_X, ALU.add))
                step(V.tensor_reduce(ecol, ecmp, AX_X, ALU.add))
                settled()
                step(V.tensor_copy(posi, pos))
                V.tensor_scalar(ecol, ecol, float(EXPERTS - 1), None, ALU.min).then_inc(s["ecol"], 1)
                settled()
                step(V.tensor_scalar(ji, posi, 7, None, ALU.logical_shift_right))
                settled()
                V.tensor_copy(jf, ji).then_inc(s["hot"], 1)
                dve.wait_ge(s["hot"], 1)
                step(V.scalar_tensor_tensor(sf, jf, -float(P), pos, ALU.mult, ALU.add))
                settled()
                for n in range(TOP_K * NT):
                    if n >= RING:
                        dve.wait_ge(s["place_ps"], n - RING + 1)
                    V.tensor_scalar(slot_hot[:, n % RING, :], iota16[:, :], sf[:, n:n + 1], None,
                                    ALU.is_equal).then_inc(s["slot_hot"], 1)
                dve.wait_ge(s["etile_ps"], 1)
                V.tensor_copy(etile[0:1, :], bank[6][0:1, 0:P]).then_inc(s["etile"], 1)
                dve.wait_ge(s["place_ps"], TOP_K * NT)
                step(V.tensor_copy(codes[:, :, :], bank[7][:, 0:TOP_K * TILES].rearrange("p (k j) -> p k j", k=TOP_K)))
                settled()
                step(V.tensor_reduce(csum, codes.rearrange("p k j -> p j k"), AX_X, ALU.add))
                settled()
                V.tensor_scalar(gidx[:, :], csum, -1.0, 0.0, ALU.add, ALU.max).then_inc(s["gidx"], 1)
                step(V.tensor_scalar(ksum, codes[:, 1, :], 0.0, float(TOKENS), ALU.is_gt, ALU.mult))
                step(V.scalar_tensor_tensor(ppres, csum, 0.0, const("spare1"), ALU.is_equal, ALU.mult))
                for k in (2, 3):
                    step(V.tensor_scalar(codes[:, k, :], codes[:, k, :], 0.0, float(k * TOKENS), ALU.is_gt, ALU.mult))
                settled()
                step(V.tensor_tensor(ksum, ksum, codes[:, 2, :], ALU.add))
                step(V.tensor_tensor(ppres, ppres, csum, ALU.add))
                settled()
                step(V.tensor_tensor(ksum, ksum, codes[:, 3, :], ALU.add))
                settled()
                V.scalar_tensor_tensor(sidx[:, :], ksum, -1.0, ppres, ALU.add, ALU.add).then_inc(s["sidx"], 1)

            def tile(s, j, b, lo):
                gu = bank[2 + b]
                dve.wait_ge(s["gu_ps"], j + 1)
                if lo >= 2:
                    dve.wait_ge(s["sig"], j - 1)
                V.tensor_scalar(gate[:, b], gu[:, 0:HID], LIMIT, None, ALU.min).then_inc(s["gate"], 1)
                V.tensor_scalar(up[:, b], gu[:, HID:GU], LIMIT, -LIMIT, ALU.min, ALU.max).then_inc(s["gu_used"], 1)
                dve.wait_ge(s["gate"], j + 1)
                dve.wait_ge(s["gu_used"], j + 1)
                V.scalar_tensor_tensor(prod[:, b], up[:, b], 1.0, gate[:, b], ALU.add, ALU.mult).then_inc(s["prod"], 1)
                dve.wait_ge(s["prod"], j + 1)
                dve.wait_ge(s["sig"], j + 1)
                if lo >= 2:
                    dve.wait_ge(s["ht_ps"], j - 1)
                V.tensor_tensor(hid[:, b], prod[:, b], sig[:, b], ALU.mult).then_inc(s["hid"], 1)

            def tile_loop(s):
                for u in range(UNROLL):
                    tile(s, u, u % 2, u)
                with dve.Fori(UNROLL, TILES - UNROLL + 1, UNROLL) as j0:
                    for u in range(UNROLL):
                        tile(s, j0 + u, u % 2, 8)

            def combine(s, i):
                dve.wait_ge(s["y_back"][i % 2], 16 * (i // 2 + 1))
                for k in range(TOP_K):
                    if k:
                        settled()
                    m = V.scalar_tensor_tensor(X[:, i, :], yc[:, i % 2, k, :], wk[:, i, k:k + 1], X[:, i, :],
                                               ALU.mult, ALU.add)
                    if k < TOP_K - 1:
                        step(m)
                    else:
                        m.then_inc(s["combined"], 1)

            def attention(s, before):
                dve.wait_ge(rows_in, 16)
                for g in range(NG):
                    for t in range(GT):
                        combine(before, g * GT + t)
                    dve.wait_ge(before["combined"], GT * (g + 1))
                    tile_stats(s, g, 0, lambda n: X[:, n, :])
                    normalise(s, 0, 2 * g + 1, g, lambda n: X[:, n, :], lambda t: xn[:, 0, t, :])
                    settled()
                    tile_stats(s, g, 1, lambda n: xn[:, 0, n % GT, :])
                    for t in range(GT):
                        step(V.tensor_tensor(X[:, g * GT + t, :], X[:, g * GT + t, :], xn[:, 0, t, :], ALU.add))
                    if g >= 1:
                        dve.wait_ge(s["xn_ps"], C * g)
                    normalise(s, 1, 2 * g + 2, g, lambda n: xn[:, 0, n % GT, :], lambda t: xn[:, 1, t, :], s["xn"])
                    for t in range(GT):
                        step(V.tensor_tensor(X[:, g * GT + t, :], X[:, g * GT + t, :], row("bout"), ALU.add))
                    for t in range(GT):
                        n = g * GT + t
                        dve.wait_ge(s["kv_ps"], n + 1)
                        if n >= 2:
                            dve.wait_ge(s["ssq"], 2 * (n - 1))
                        V.tensor_tensor(kv[:, t % 2, :], bank[2 + n % 2][:, :], row("bkv"), ALU.add).then_inc(s["kv"], 1)
                        dve.wait_ge(s["kv"], n + 1)
                        both = kv[:, t % 2, :].rearrange("p (m d) -> p m d", m=2)
                        half = t % 2
                        cos = const("cos")[:, half * ROT:(half + 1) * ROT].unsqueeze(1).to_broadcast([P, 2, ROT])
                        sin = const("sin")[:, half * ROT:(half + 1) * ROT].unsqueeze(1).to_broadcast([P, 2, ROT])
                        step(V.tensor_tensor(rot, both[:, :, 0:ROT], cos, ALU.mult))
                        step(V.tensor_tensor(rots, both[:, :, 0:ROT], sin, ALU.mult))
                        settled()
                        step(V.tensor_tensor(rotd[:, :, 0:HALF], rot[:, :, 0:HALF], rots[:, :, HALF:ROT], ALU.add))
                        step(V.tensor_tensor(rotd[:, :, HALF:ROT], rot[:, :, HALF:ROT], rots[:, :, 0:HALF], ALU.add))
                        settled()
                        if t == 0 and g >= 1:
                            dve.wait_ge(s["a_ps"], g)
                        step(V.tensor_tensor(kvprod[:, t, ROT:D], both[:, 0, ROT:D], both[:, 1, ROT:D], ALU.mult))
                        V.tensor_tensor(kvprod[:, t, 0:ROT], rotd[:, 0, :], rotd[:, 1, :], ALU.mult).then_inc(s["kvprod"], 1)
                    dve.wait_ge(s["norm"], g + 1)
                    if g >= 1:
                        dve.wait_ge(s["a_ps"], g)
                    step(V.tensor_tensor(rkv[:, :], nrm[:, :, 0], nrm[:, :, 1], ALU.mult))
                    settled()
                    V.reciprocal(rkv[:, :], rkv[:, :]).then_inc(s["rkv"], 1)
                    dve.wait_ge(s["a_ps"], g + 1)
                    V.tensor_scalar(amix.rearrange("p b c -> p (b c)"), bank[4][:, 0:2 * C], 0.5, 0.5, ALU.mult,
                                    ALU.add).then_inc(s["amix"], 1)
                    dve.wait_ge(s["amix"], g + 1)
                    if g >= 1:
                        dve.wait_ge(s["o_ps"], GT * g)
                    for b in range(2):
                        for c in range(C):
                            m = V.tensor_scalar(aw[:, b, c, :], wout[:, c, :], amix[:, b, c:c + 1], None, ALU.mult)
                            if c < C - 1:
                                step(m)
                            else:
                                m.then_inc(s["aw"], 1)
                    for t in range(GT):
                        n = g * GT + t
                        dve.wait_ge(s["o_ps"], n + 1)
                        V.tensor_tensor(X[:, n, :], bank[7][:, 0:D], X[:, n, :], ALU.add).then_inc(s["x2"], 1)

            dve.wait_ge(const_in, 16)
            V.tensor_copy(iota16[:, :], const("iota")).then_inc(iota_set, 1)
            dve.wait_ge(bias_in, 16)
            step(V.tensor_copy(bpart[:, 0, :], bsrc))
            settled()
            step(V.tensor_tensor(bres, bsrc, bpart[:, 0, :], ALU.subtract))
            settled()
            step(V.tensor_copy(bpart[:, 1, :], bres))
            settled()
            step(V.tensor_tensor(bres2, bres, bpart[:, 1, :], ALU.subtract))
            settled()
            V.tensor_copy(bpart[:, 2, :], bres2).then_inc(bias_split, 1)
            dve.wait_ge(bias_split, 1)
            dve.wait_ge(rows_in, 16)
            dve.wait_ge(iota_set, 1)
            ffn_front(ffn[0], 0)
            routing(ffn[0])
            tile_loop(ffn[0])
            attention(att, ffn[0])
            dve.wait_ge(att["x2"], NT)
            ffn_front(ffn[1], 1)
            routing(ffn[1])
            tile_loop(ffn[1])
            for i in range(NT):
                combine(ffn[1], i)


def _constants():
    p = np.arange(P)
    c = np.zeros((P, CONST_W), np.float32)

    def put(name, v):
        at, w = CONST[name]
        c[:, at:at + w] = np.asarray(v, np.float32).reshape(-1, w) if np.ndim(v) else v

    put("ident", np.eye(P))
    put("lowm", (p[:, None] < p[None, :]).astype(np.float32) - 1.0)
    put("iota", np.tile(p, (P, 1)))
    put("seg", np.tile((np.arange(EXPERTS * NT) % NT != 0), (P, 1)))
    put("tid1", np.arange(NT)[None, :] * P + p[:, None] + 1)
    put("part128", p[:, None] * P)
    put("spare1", TOP_K * TOKENS + np.arange(TILES)[None, :] * P + p[:, None] + 1)
    inv = (1.0 / 10000.0 ** (np.arange(0, ROT, 2, dtype=np.float32) / np.float32(ROT))).astype(np.float32)
    ang = (np.arange(SEQ, dtype=np.float32)[:, None] * inv[None, :]).astype(np.float32)
    cos, sin = np.cos(ang), np.sin(ang)
    put("cos", np.concatenate([np.concatenate([cos[h * P:(h + 1) * P]] * 2, 1) for h in range(2)], 1))
    put("sin", np.concatenate([np.concatenate([sin[h * P:(h + 1) * P], -sin[h * P:(h + 1) * P]], 1) for h in range(2)], 1))
    return c


def kernel(**inputs):
    import concourse.bacc as _bacc
    from concourse.bass_utils import run_bass_kernel_spmd as _run

    a = {k[3:]: np.asarray(v) for k, v in inputs.items()}
    perm = np.concatenate([np.arange(0, ROT, 2), np.arange(1, ROT, 2), np.arange(ROT, D)])
    perm3 = np.concatenate([perm, D + perm, 2 * D + perm])

    def chunks(w):
        return w.reshape(C, P, -1).transpose(1, 0, 2)

    w_in = chunks(a["attn_W_in"][:, perm3])
    w_out = chunks(a["attn_W_out"][perm, :])
    b_in = a["attn_b_in"][perm3]
    w_gu = a["ffn_gate_up_proj"].reshape(EXPERTS, C, P, HID, 2).transpose(2, 0, 1, 4, 3).reshape(P, EXPERTS, C, GU)
    w_dn = a["ffn_down_proj"].reshape(EXPERTS, C, P, D).transpose(2, 0, 1, 3)
    b_gu = a["ffn_gate_up_proj_bias"].reshape(EXPERTS, HID, 2).transpose(0, 2, 1).reshape(EXPERTS, GU)
    bias = np.concatenate([b_gu, a["ffn_down_proj_bias"]], 1).reshape(P, BCOL)
    rows = np.concatenate([a["ffn_router_bias"], b_in[D:], a["attn_b_out"]])
    pweights = np.concatenate([
        chunks(a["ffn_router_weight"].T).reshape(P, -1), a["attn_gamma"].reshape(C, P).T,
        a["attn_beta"].reshape(C, P).T, b_in[:D].reshape(C, P).T], 1)
    sent = {"x": a["attn_X"].reshape(TOKENS, D), "consts": _constants(), "rows": rows, "pweights": pweights,
            "w_in": w_in, "w_out": w_out, "w_gu": w_gu, "w_down": w_dn, "bias": bias}
    nc = _bacc.Bacc("TRN2", target_bir_lowering=False, num_devices=1)
    arrays, args = {}, []
    for name, v in sent.items():
        v = np.ascontiguousarray(v)
        arrays[f"in_{name}"] = v
        args.append(nc.dram_tensor(f"in_{name}", v.shape, mybir.dt.from_np(v.dtype), kind="ExternalInput").ap())
    args.append(nc.dram_tensor("out", [TOKENS, D], F32, kind="ExternalOutput").ap())
    macaron_kernel(nc, *args)
    r = _run(nc, [arrays], core_ids=[0])
    return r.results[0]["out"].reshape(BATCH, SEQ, D)
```

```python
from contextlib import ExitStack

import numpy as np
import concourse.bass as bass
from concourse import mybir

ALU = mybir.AluOpType
ACT = mybir.ActivationFunctionType
F32 = mybir.dt.float32
F16 = mybir.dt.float16
BF16 = mybir.dt.bfloat16
I32 = mybir.dt.int32
U32 = mybir.dt.uint32
AX_X = mybir.AxisListType.X

P = 128
BATCH, SEQ, D = 8, 256, 256
TOKENS = BATCH * SEQ
NT = TOKENS // P
GT = 4
NG = NT // GT
C = D // P
EXPERTS, TOP_K = 16, 4
HID = 256
GU = 2 * HID
UNROLL = 4
YL = 6
LATE = 2
TILES = TOKENS * TOP_K // P + EXPERTS - 1
TILES = -(-TILES // UNROLL) * UNROLL
ROT = D // 2
HALF = ROT // 2
LIMIT, ALPHA = 7.0, 1.702
EPS = 1e-5
BROW = GU + D
BATT = EXPERTS * BROW
BTOT = BATT + 3 * D
BCOL = BTOT // P
XBUF = 3

CONST = {}
for _n, _w in (("ident", P), ("iota", EXPERTS), ("seg", EXPERTS * NT), ("tid1", NT), ("part128", 1),
               ("spare1", TILES), ("cos", 2 * ROT), ("sin", 2 * ROT)):
    CONST[_n] = (sum(w for _, w in CONST.values()), _w)
CONST_W = sum(w for _, w in CONST.values())
PW = {"rw": (0, C * EXPERTS), "gamma": (C * EXPERTS, C), "beta": (C * EXPERTS + C, C), "bq": (C * EXPERTS + 2 * C, C)}
PW_W = C * EXPERTS + 3 * C


def macaron_kernel(nc, x, consts, consts16, rbias, pweights, w_in, w_out, w_gu, w_down, bias, out):
    x_v = x.rearrange("(i p) d -> p i d", p=P)
    out_v = out.rearrange("(i p) d -> p i d", p=P)
    xn_dram = nc.dram_tensor("xn_dram", [TOKENS, D], F32, kind="Internal").ap()
    y_dram = nc.dram_tensor("y_dram", [TOP_K * TOKENS + TILES * P, D], F32, kind="Internal").ap()
    y_v = y_dram[0:TOP_K * TOKENS, :].rearrange("(k i p) d -> p k i d", k=TOP_K, p=P)
    bias_dram = nc.dram_tensor("bias_dram", [3, BTOT], BF16, kind="Internal").ap()
    xn_v = xn_dram.rearrange("(i p) d -> p i d", p=P)

    with ExitStack() as ctx:
        def sb(name, shape, dt=F32):
            return ctx.enter_context(nc.sbuf_tensor(name, shape, dt))

        def sem(name):
            return ctx.enter_context(nc.semaphore(name))

        bank = [ctx.enter_context(nc.psum_tensor(f"bank{n}", [P, 512], F32)) for n in range(8)]

        wgu = sb("wgu", [P, EXPERTS, C, GU])
        wdn = sb("wdn", [P, EXPERTS, C, D])
        biases = sb("biases", [P, BTOT], BF16)
        brow = biases[:, 0:BATT].rearrange("p (e n) -> p e n", e=EXPERTS)
        bkv = biases[:, BATT:BATT + 2 * D]
        bout = biases[:, BATT + 2 * D:BTOT]
        X = sb("X", [P, NT, D])
        xnT = sb("xnT", [P, 2, C, GT * P])
        win = sb("win", [P, C, 3 * D])
        wout = sb("wout", [P, C, D])
        cst = sb("cst", [P, CONST_W])
        rb = sb("rb", [P, EXPERTS])
        pw = sb("pw", [P, PW_W])
        xn = sb("xn", [P, XBUF, GT, D])
        onesb = sb("onesb", [P, P], BF16)
        cst16 = sb("cst16", [P, 2 * P], F16)
        lowm, iota16 = cst16[:, 0:P], cst16[:, P:2 * P]
        epsc = sb("epsc", [P, 1])
        stats = sb("stats", [P, 3, GT, 6])
        mv = sb("mv", [P, 3, GT, 2])
        rstd = sb("rstd", [P, 3, GT])
        tops = sb("tops", [P, NT, 8])
        wk = sb("wk", [P, NT, TOP_K])
        gidx = sb("gidx", [P, TILES], U32)
        sidx = sb("sidx", [P, TILES], U32)
        etile = sb("etile", [1, P], I32)
        gcol = sb("gcol", [P, UNROLL], U32)
        scol = sb("scol", [P, UNROLL], U32)
        WORK = 24 * 256
        work = sb("work", [P, WORK])

        def wk_area(at, *shape):
            n = int(np.prod(shape))
            names = "abc"[:len(shape)]
            v = work[:, at:at + n]
            if len(shape) == 1:
                return v
            return v.rearrange(f"p ({' '.join(names)}) -> p {' '.join(names)}",
                               **{names[i]: shape[i] for i in range(len(shape))})

        xg = wk_area(0, 4, D)
        yb = wk_area(4 * D, 4, D)
        xT = wk_area(8 * D, 2, D)
        hT = wk_area(10 * D, 2, D)
        gate = wk_area(12 * D, 2, D)
        up = wk_area(14 * D, 2, D)
        prod = wk_area(16 * D, 2, D)
        sig = wk_area(18 * D, 2, D)
        hid = wk_area(20 * D, 2, D)
        yc = wk_area(0, 2, TOP_K, D)
        yl = wk_area(0, YL, TOP_K, D)
        logits = sb("logits", [P, NT, EXPERTS])
        topi = sb("topi", [P, NT, 8], U32)
        topif = wk_area(256, NT, TOP_K)
        hot = wk_area(512, TOP_K, EXPERTS, NT)
        hot2 = wk_area(1536, 2, EXPERTS * NT)
        mask = wk_area(2048, EXPERTS * NT // 2).bitcast(F16)
        pre = wk_area(2304, EXPERTS * NT // 2).bitcast(F16)
        posall = wk_area(2560, EXPERTS, NT)
        hotpos = wk_area(2816, TOP_K, EXPERTS, NT)
        pos = wk_area(3840, TOP_K * NT)
        jf = wk_area(3904, TOP_K * NT)
        sf = wk_area(3968, TOP_K * NT)
        posi = wk_area(4032, TOP_K * NT).bitcast(I32)
        ji = wk_area(4096, TOP_K * NT).bitcast(I32)
        cnti = wk_area(4160, EXPERTS).bitcast(I32)
        nt128 = wk_area(4176, EXPERTS).bitcast(I32)
        tend = wk_area(4192, EXPERTS)
        base = wk_area(4208, EXPERTS)
        ecmp = wk_area(4224, EXPERTS)
        ecol = wk_area(4240, 1)
        wsum = wk_area(448, NT)
        wrec = wk_area(464, NT)
        codes = wk_area(4244, TOP_K, TILES)
        csum = wk_area(4564, TILES)
        ksum = wk_area(4644, TILES)
        ppres = wk_area(4724, TILES)
        RING = 8
        slot_hot = wk_area(4804, RING * P // 2).bitcast(F16).rearrange("p (r s) -> p r s", r=RING)
        tile_hot = wk_area(4804 + RING * P // 2, RING * TILES // 2).bitcast(F16).rearrange("p (r s) -> p r s", r=RING)
        kv = wk_area(2048, GT, 2 * D)
        rot = wk_area(4096, 2, ROT)
        rots = wk_area(4352, 2, 2 * ROT)
        kvprod = wk_area(4864, GT, D)
        junk = wk_area(5888, D)
        aw = sb("aw", [P, 2, C, D])
        qT = sb("qT", [P, C, GT * P])
        ssq = sb("ssq", [P, GT, 2])
        nrm = sb("nrm", [P, GT, 2])
        rkv = sb("rkv", [P, GT])
        amix = sb("amix", [P, 2, C])
        BIAS_AT = WORK - 5 * BCOL
        bsrc = wk_area(BIAS_AT, BCOL)
        bres = wk_area(BIAS_AT + BCOL, BCOL)
        bres2 = wk_area(BIAS_AT + 2 * BCOL, BCOL)
        bpart = wk_area(BIAS_AT + 3 * BCOL, 3 * BCOL // 2).bitcast(BF16).rearrange("p (n j) -> p n j", n=3)

        def const(name):
            at, w = CONST[name]
            return cst[:, at:at + w]

        def pwt(name):
            at, w = PW[name]
            return pw[:, at:at + w]

        rw = pwt("rw").rearrange("p (c e) -> p c e", c=C)

        const_in, rbias_in, pw_in, bias_in, attw_in, w_loaded = map(
            sem, ("const_in", "rbias_in", "pw_in", "bias_in", "attw_in", "w_loaded"))
        x_in = [sem(f"x_in{g}") for g in range(NG)]
        bias_split, bias_stored, bias_rows, bias_zero, ones_set = map(
            sem, ("bias_split", "bias_stored", "bias_rows", "bias_zero", "ones_set"))
        dve_step = sem("dve_step")
        out_stored = sem("out_stored")

        def signals(tag, names, **lists):
            one = {n: sem(f"{tag}_{n}") for n in names.split()}
            one.update({n: [sem(f"{tag}_{n}{m}") for m in range(count)] for n, count in lists.items()})
            return one

        FFN = ("var std xn xn_ps xnT logit_ps logit wexp_in wexp pre cnt_ps hot slot_hot tile_hot tile_hot_pool place_ps cols gcol scol ecol etile_ps "
               "etile gidx sidx xt_ps xt gu_ps gate gu_used prod sig hid ht_ps ht y_ps y")
        ffn = [signals(f"ffn{f}", FFN + " combined", xn_stored=XBUF, gathered=UNROLL, scattered=UNROLL,
                       y_back=YL)
               for f in range(2)]
        att = signals("att", "var std xin xn xn_ps xnT kv_ps kv ssq norm rots xsum kvpass kvprod rkv a_ps amix aw q_ps qT o_ps x2")

        block = ctx.enter_context(nc.Block())

        @block.sync
        def _(sp):
            sp.dma_start(cst[:, :], consts).then_inc(const_in, 16)
            sp.dma_start(cst16[:, :], consts16).then_inc(const_in, 16)
            for g in range(NG):
                sp.dma_start(X[:, g * GT:(g + 1) * GT, :], x_v[:, g * GT:(g + 1) * GT, :]).then_inc(x_in[g], 16)
            sp.dma_start(pw[:, :], pweights).then_inc(pw_in, 16)
            sp.dma_start(rb[:, :], rbias.partition_broadcast(P)).then_inc(rbias_in, 16)
            sp.dma_start(bsrc, bias).then_inc(bias_in, 16)
            for g in range(NG):
                for e in range(g * EXPERTS // NG, (g + 1) * EXPERTS // NG):
                    sp.dma_start(wgu[:, e], w_gu[:, e]).then_inc(w_loaded, 16)
                    sp.dma_start(wdn[:, e], w_down[:, e]).then_inc(w_loaded, 16)
                sp.wait_ge(ffn[0]["xn_stored"][g % XBUF], 16 * (g // XBUF + 1))
            sp.dma_start(win[:, :, :], w_in).then_inc(attw_in, 16)
            sp.dma_start(wout[:, :, :], w_out).then_inc(attw_in, 16)
            for f in range(2):
                ring, buf = ((2, yc), (YL, yl))[f]
                for u in range(UNROLL):
                    sp.wait_ge(ffn[f]["scattered"][u], 16 * TILES // UNROLL)
                for i in range(NT):
                    if i >= ring:
                        sp.wait_ge(ffn[f]["combined"], i - ring + 1)
                    sp.dma_start(buf[:, i % ring], y_v[:, :, i, :]).then_inc(ffn[f]["y_back"][i % ring], 16)
            for i in range(NT):
                sp.wait_ge(ffn[1]["combined"], i + 1)
                sp.dma_start(out_v[:, i, :], X[:, i, :]).then_inc(out_stored, 16)
            sp.wait_ge(out_stored, 16 * NT)

        @block.gpsimd
        def _(pool):
            nc.gpsimd.memset(onesb[:, :], 1.0).then_inc(ones_set, 1)
            nc.gpsimd.memset(epsc[:, :], EPS).then_inc(ones_set, 1)
            nc.gpsimd.memset(biases[:, :], 0.0).then_inc(bias_zero, 1)

            def tile_hots(s):
                pool.wait_ge(const_in, 32)
                pool.wait_ge(s["hot"], 1)
                for n in range(2, TOP_K * NT, 3):
                    if n >= RING:
                        pool.wait_ge(s["place_ps"], n - RING + 1)
                    nc.gpsimd.tensor_scalar(tile_hot[:, n % RING, :], iota16[:, 0:TILES], jf[:, n:n + 1],
                                            const("tid1")[:, n % NT:n % NT + 1], ALU.is_equal,
                                            ALU.mult).then_inc(s["tile_hot_pool"], 1)

            def tile(s, j, u, lo):
                if lo + UNROLL < TILES:
                    pool.wait_ge(s["xt_ps"], j + 1)
                    gather(s, j + UNROLL, u)
                if lo >= LATE:
                    scatter(s, j - LATE, (u - LATE) % UNROLL, lo - LATE)

            def copy_cols(s, dst, src, signal, count):
                nc.gpsimd.tensor_copy(dst, src).then_inc(signal, 1)
                pool.wait_ge(signal, count)
                pool.sem_inc(s["cols"], 1)

            def gather(s, j, u):
                copy_cols(s, gcol[:, u:u + 1], gidx[:, bass.ds(j, 1)], s["gcol"], j + 1)
                nc.gpsimd.indirect_dma_start(
                    out=xg[:, u, :], out_offset=None, in_=xn_dram,
                    in_offset=bass.IndirectOffsetOnAxis(ap=gcol[:, u:u + 1], axis=0)).then_inc(s["gathered"][u], 16)

            def scatter(s, j, u, lo):
                if lo >= UNROLL:
                    pool.wait_ge(s["scattered"][u], 4 * j - 4 * u)
                pool.wait_ge(s["y"], j + 1)
                copy_cols(s, scol[:, u:u + 1], sidx[:, bass.ds(j, 1)], s["scol"], j + 1)
                nc.gpsimd.indirect_dma_start(
                    out=y_dram, out_offset=bass.IndirectOffsetOnAxis(ap=scol[:, u:u + 1], axis=0),
                    in_=yb[:, u, :], in_offset=None).then_inc(s["scattered"][u], 16)

            pool.wait_ge(bias_split, 1)
            nc.gpsimd.dma_start(bias_dram.rearrange("n (p j) -> p n j", p=P), bpart).then_inc(bias_stored, 16)
            pool.wait_ge(bias_stored, 16)
            pool.wait_ge(bias_zero, 1)
            nc.gpsimd.dma_start(biases[0:3, :], bias_dram).then_inc(bias_rows, 16)
            def attention(s):
                for g in range(NG + 1):
                    for t in range(GT):
                        n = (g - 1) * GT + t
                        if g == 0:
                            continue
                        half = t % 2
                        pool.wait_ge(s["kv"], n + 1)
                        if n >= 2:
                            pool.wait_ge(s["kvprod"], n - 1)
                        k_and_v = kv[:, t, :].rearrange("p (m d) -> p m d", m=2)
                        sin = const("sin")[:, half * ROT:(half + 1) * ROT].unsqueeze(1).to_broadcast([P, 2, ROT])
                        nc.gpsimd.tensor_tensor(rots[:, n % 2, :].rearrange("p (m d) -> p m d", m=2),
                                                k_and_v[:, :, 0:ROT], sin, ALU.mult).then_inc(s["rots"], 1)
                        if t == 0 and g >= 2:
                            pool.wait_ge(s["a_ps"], g - 1)
                        nc.gpsimd.tensor_tensor(kvprod[:, t, ROT:D], k_and_v[:, 0, ROT:D], k_and_v[:, 1, ROT:D],
                                                ALU.mult).then_inc(s["kvpass"], 1)
                    if g < NG:
                        pool.wait_ge(s["xin"], g + 1)
                        for t in range(GT):
                            n = g * GT + t
                            nc.gpsimd.tensor_tensor(X[:, n, :], X[:, n, :], xn[:, 0, t, :],
                                                    ALU.add).then_inc(s["xsum"], 1)

            for f in range(2):
                s = ffn[f]
                if f == 1:
                    attention(att)
                tile_hots(s)
                pool.wait_ge(s["gidx"], 1)
                pool.wait_ge(s["sidx"], 1)
                for g in range(NG):
                    b = g % XBUF if f == 0 else 2
                    pool.wait_ge(s["xn_stored"][b], 16 * (g // XBUF + 1 if f == 0 else g + 1))
                for u in range(UNROLL):
                    gather(s, u, u)
                for u in range(2 * UNROLL):
                    tile(s, u, u % UNROLL, u)
                with pool.Fori(2 * UNROLL, TILES - 2 * UNROLL + 1, UNROLL) as j0:
                    for u in range(UNROLL):
                        tile(s, j0 + u, u, 2 * UNROLL)
                for u in range(UNROLL):
                    tile(s, TILES - UNROLL + u, u, TILES - UNROLL + u)
                for j in range(TILES - LATE, TILES):
                    scatter(s, j, j % UNROLL, j)

        @block.scalar
        def _(act):
            act.wait_ge(ones_set, 2)

            def std_of(s, count, b):
                act.wait_ge(s["var"], count)
                nc.scalar.activation(rstd[:, b, :], mv[:, b, :, 1], ACT.Sqrt, bias=epsc[:, 0:1]).then_inc(s["std"], 1)

            def store_xn(s, g, xb):
                act.wait_ge(s["xn"], g + 1)
                nc.scalar.dma_start(xn_v[:, g * GT:(g + 1) * GT, :], xn[:, xb]).then_inc(s["xn_stored"][xb], 16)

            def take_xnT(s, g, b, tb):
                for c in range(C):
                    act.wait_ge(s["xn_ps"], C * g + c + 1)
                    nc.scalar.activation(xnT[:, tb, c, :], bank[b + c][:, :], ACT.Copy).then_inc(s["xnT"], 1)

            def ffn_front(s):
                std_of(s, 1, 0)
                for g in range(NG):
                    if g + 1 < NG:
                        std_of(s, g + 2, (g + 1) % 2)
                    store_xn(s, g, g % XBUF)
                    if g >= 2:
                        act.wait_ge(s["logit_ps"], g - 1)
                    take_xnT(s, g, C * (g % 2), g % 2)

            def weights_exp(s):
                act.wait_ge(s["wexp_in"], 1)
                nc.scalar.activation(wk[:, :, :], wk[:, :, :], ACT.Exp).then_inc(s["wexp"], 1)

            def tile(s, j, j0, u, nxt, prv, prv2, lo):
                b = u % 2
                if nxt:
                    take_xt(s, j + 1, (u + 1) % 2, lo + 1)
                act.wait_ge(s["gate"], j + 1)
                if lo >= 2:
                    act.wait_ge(s["hid"], j - 1)
                nc.scalar.activation(sig[:, b], gate[:, b], ACT.Sigmoid, scale=ALPHA).then_inc(s["sig"], 1)
                if prv:
                    take_ht(s, j - 1, (u + 1) % 2, lo - 1)
                if prv2:
                    take_y(s, j - 2, (u + 2) % 4, lo - 2)

            def take_xt(s, j, b, lo):
                act.wait_ge(s["xt_ps"], j + 1)
                if lo >= 2:
                    act.wait_ge(s["gu_ps"], j - 1)
                nc.scalar.activation(xT[:, b], bank[b][:, 0:D], ACT.Copy).then_inc(s["xt"], 1)

            def take_ht(s, j, b, lo):
                act.wait_ge(s["ht_ps"], j + 1)
                if lo >= 2:
                    act.wait_ge(s["y_ps"], j - 1)
                nc.scalar.activation(hT[:, b], bank[4 + b][:, 0:D], ACT.Copy).then_inc(s["ht"], 1)

            def take_y(s, j, u, lo):
                act.wait_ge(s["y_ps"], j + 1)
                if lo >= 4:
                    act.wait_ge(s["scattered"][u], 4 * j - 4 * u)
                nc.scalar.activation(yb[:, u], bank[6 + u % 2][:, 0:D], ACT.Copy).then_inc(s["y"], 1)

            def tile_loop(s):
                take_xt(s, 0, 0, 0)
                for u in range(2 * UNROLL):
                    tile(s, u, None, u % UNROLL, True, u >= 1, u >= 2, u)
                with act.Fori(2 * UNROLL, TILES - 2 * UNROLL + 1, UNROLL) as j0:
                    for u in range(UNROLL):
                        tile(s, j0 + u, j0, u, True, True, True, 8)
                for u in range(UNROLL):
                    j = TILES - UNROLL + u
                    tile(s, j, None, u, u < UNROLL - 1, True, True, j)
                take_ht(s, TILES - 1, 1, TILES - 1)
                take_y(s, TILES - 2, 2, TILES - 2)
                take_y(s, TILES - 1, 3, TILES - 1)

            def take_kv(s, g, t):
                n = g * GT + t
                act.wait_ge(s["kv_ps"], n + 1)
                if g >= 1:
                    act.wait_ge(s["kvprod"], GT * g)
                    act.wait_ge(s["kvpass"], GT * g)
                nc.scalar.activation(kv[:, t, :], bank[2 + n % 2][:, :], ACT.Copy).then_inc(s["kv"], 1)
                if t == 0 and g >= 1:
                    act.wait_ge(s["norm"], g)
                for m in range(2):
                    if n or m:
                        act.wait_ge(s["ssq"], 2 * n + m)
                    nc.scalar.activation(junk, bank[2 + n % 2][:, m * D:(m + 1) * D], ACT.Square,
                                         accum_out=ssq[:, t, m:m + 1]).then_inc(s["ssq"], 1)

            def attention(s, front):
                for g in range(NG + 1):
                    if g < NG:
                        std_of(s, 2 * g + 1, 0)
                        std_of(s, 2 * g + 2, 1)
                        if g >= 1:
                            act.wait_ge(s["q_ps"], C * g)
                        for c in range(C):
                            act.wait_ge(s["xn_ps"], C * g + c + 1)
                            nc.scalar.activation(xnT[:, 0, c, :], bank[c][:, :], ACT.Identity,
                                                 bias=pwt("beta")[:, c:c + 1],
                                                 scale=pwt("gamma")[:, c:c + 1]).then_inc(s["xnT"], 1)
                        take_kv(s, g, 0)
                    if g >= 1:
                        std_of(front, g, 2)
                    if g < NG:
                        for t in range(1, GT):
                            take_kv(s, g, t)
                    if g >= 1:
                        store_xn(front, g - 1, 2)
                        if g >= 2:
                            act.wait_ge(front["logit_ps"], g - 1)
                        take_xnT(front, g - 1, 0, 1)
                    if g < NG:
                        act.wait_ge(s["ssq"], 2 * GT * (g + 1))
                        if g >= 1:
                            act.wait_ge(s["rkv"], g)
                        nc.scalar.activation(nrm[:, :, :], ssq[:, :, :], ACT.Sqrt).then_inc(s["norm"], 1)
                        for c in range(C):
                            act.wait_ge(s["q_ps"], C * g + c + 1)
                            if g >= 1:
                                act.wait_ge(s["o_ps"], GT * g)
                            nc.scalar.activation(qT[:, c, :], bank[5 + c][:, :], ACT.Identity,
                                                 bias=pwt("bq")[:, c:c + 1]).then_inc(s["qT"], 1)

            act.wait_ge(pw_in, 16)
            ffn_front(ffn[0])
            weights_exp(ffn[0])
            tile_loop(ffn[0])
            attention(att, ffn[1])
            weights_exp(ffn[1])
            tile_loop(ffn[1])

        @block.tensor
        def _(pe):
            ident = const("ident")

            def group_transposes(s, g, b, xb):
                for c in range(C):
                    for t in range(GT):
                        mm = nc.tensor.transpose(bank[b + c][:, t * P:(t + 1) * P],
                                                 xn[:, xb, t, c * P:(c + 1) * P], ident)
                    mm.then_inc(s["xn_ps"], 1)

            def router(s, g, b, tb):
                pe.wait_ge(s["xnT"], C * (g + 1))
                for t in range(GT):
                    for c in range(C):
                        mm = nc.tensor.matmul(bank[b][:, t * EXPERTS:(t + 1) * EXPERTS],
                                              xnT[:, tb, c, t * P:(t + 1) * P], rw[:, c, :],
                                              start=(c == 0), stop=(c == C - 1))
                mm.then_inc(s["logit_ps"], 1)

            def ffn_front(s):
                for g in range(NG):
                    pe.wait_ge(s["xn"], g + 1)
                    if g >= 2:
                        pe.wait_ge(s["xnT"], C * (g - 1))
                    group_transposes(s, g, C * (g % 2), g % XBUF)
                    if g >= 2:
                        pe.wait_ge(s["logit"], g - 1)
                    router(s, g, 4 + g % 2, g % 2)

            def routing(s):
                pe.wait_ge(s["pre"], 1)
                nc.tensor.matmul(bank[6][:, 0:EXPERTS * NT], onesb[:, :], pre, start=True, stop=False)
                nc.tensor.matmul(bank[6][:, 0:EXPERTS * NT], lowm, mask, start=False, stop=True)
                nc.tensor.matmul(bank[6][:, EXPERTS * NT:EXPERTS * NT + EXPERTS], onesb[:, :],
                                 pre.rearrange("p (e i) -> p e i", e=EXPERTS)[:, :, NT - 1],
                                 start=True, stop=True).then_inc(s["cnt_ps"], 1)
                pe.wait_ge(s["ecol"], 1)
                nc.tensor.matmul(bank[6][0:1, 0:P], ecol, ident, start=True, stop=True).then_inc(s["etile_ps"], 1)
                for n in range(TOP_K * NT):
                    pe.wait_ge(s["slot_hot"], n + 1)
                    if n % 3 == 2:
                        pe.wait_ge(s["tile_hot_pool"], n // 3 + 1)
                    else:
                        pe.wait_ge(s["tile_hot"], n - n // 3 + 1)
                    k, i = divmod(n, NT)
                    nc.tensor.matmul(bank[7][:, k * TILES:(k + 1) * TILES], slot_hot[:, n % RING, :],
                                     tile_hot[:, n % RING, :], start=(i == 0),
                                     stop=(i == NT - 1)).then_inc(s["place_ps"], 1)

            def turn_x(s, j, u, lo):
                pe.wait_ge(s["gathered"][u], 4 * j - 4 * u + 16)
                if lo >= 2:
                    pe.wait_ge(s["xt"], j - 1)
                for c in range(C):
                    mm = nc.tensor.transpose(bank[u % 2][:, c * P:(c + 1) * P], xg[:, u, c * P:(c + 1) * P], ident)
                mm.then_inc(s["xt_ps"], 1)

            def gate_up(s, j, b, lo):
                e = pe.value_load(etile[0:1, bass.ds(j, 1)], min_val=0, max_val=EXPERTS - 1)
                pe.wait_ge(s["xt"], j + 1)
                if lo >= 2:
                    pe.wait_ge(s["gu_used"], j - 1)
                acc = bank[2 + b][:, :]
                nc.tensor.matmul(acc, onesb[:, :], brow[:, bass.ds(e, 1), 0:GU].rearrange("p o n -> p (o n)"),
                                 start=True, stop=False)
                for c in range(C):
                    mm = nc.tensor.matmul(acc, xT[:, b, c * P:(c + 1) * P],
                                          wgu[:, bass.ds(e, 1), c, :].rearrange("p o n -> p (o n)"),
                                          start=False, stop=(c == C - 1))
                mm.then_inc(s["gu_ps"], 1)

            def turn_h(s, j, b, lo):
                pe.wait_ge(s["hid"], j + 1)
                if lo >= 2:
                    pe.wait_ge(s["ht"], j - 1)
                for c in range(C):
                    mm = nc.tensor.transpose(bank[4 + b][:, c * P:(c + 1) * P], hid[:, b, c * P:(c + 1) * P], ident)
                mm.then_inc(s["ht_ps"], 1)

            def down(s, j, b, lo):
                e = pe.value_load(etile[0:1, bass.ds(j, 1)], min_val=0, max_val=EXPERTS - 1)
                pe.wait_ge(s["ht"], j + 1)
                if lo >= 2:
                    pe.wait_ge(s["y"], j - 1)
                acc = bank[6 + b][:, 0:D]
                nc.tensor.matmul(acc, onesb[:, :], brow[:, bass.ds(e, 1), GU:BROW].rearrange("p o n -> p (o n)"),
                                 start=True, stop=False)
                for c in range(C):
                    mm = nc.tensor.matmul(acc, hT[:, b, c * P:(c + 1) * P],
                                          wdn[:, bass.ds(e, 1), c, :].rearrange("p o n -> p (o n)"),
                                          start=False, stop=(c == C - 1))
                mm.then_inc(s["y_ps"], 1)

            def tile(s, j, u, nxt, prv, prv2, lo):
                if nxt:
                    turn_x(s, j + 1, (u + 1) % UNROLL, lo + 1)
                gate_up(s, j, u % 2, lo)
                if prv:
                    turn_h(s, j - 1, (u + 1) % 2, lo - 1)
                if prv2:
                    down(s, j - 2, u % 2, lo - 2)

            def tile_loop(s, first):
                pe.wait_ge(s["etile"], 1)
                if first:
                    pe.wait_ge(w_loaded, 32 * EXPERTS)
                    pe.wait_ge(bias_rows, 16)
                turn_x(s, 0, 0, 0)
                for u in range(UNROLL):
                    tile(s, u, u, True, u >= 1, u >= 2, u)
                with pe.Fori(UNROLL, TILES - 2 * UNROLL + 1, UNROLL) as j0:
                    for u in range(UNROLL):
                        tile(s, j0 + u, u, True, True, True, 8)
                for u in range(UNROLL):
                    j = TILES - UNROLL + u
                    tile(s, j, u, u < UNROLL - 1, True, True, j)
                turn_h(s, TILES - 1, 1, TILES - 1)
                down(s, TILES - 2, 0, TILES - 2)
                down(s, TILES - 1, 1, TILES - 1)

            def mix(s, g):
                pe.wait_ge(s["rkv"], g + 1)
                pe.wait_ge(s["kvprod"], GT * (g + 1))
                pe.wait_ge(s["kvpass"], GT * (g + 1))
                for b in range(2):
                    for c in range(C):
                        for h in range(2):
                            t = 2 * b + h
                            mm = nc.tensor.matmul(bank[4][:, 2 * b + c:2 * b + c + 1],
                                                  kvprod[:, t, c * P:(c + 1) * P], rkv[:, t:t + 1],
                                                  start=(h == 0), stop=(h == 1))
                mm.then_inc(s["a_ps"], 1)

            def project(s, g):
                for t in range(GT):
                    n = g * GT + t
                    if t % 2 == 0:
                        pe.wait_ge(s["aw"], 2 * g + t // 2 + 1)
                    if t == 0:
                        pe.wait_ge(s["qT"], C * (g + 1))
                    if n >= 1:
                        pe.wait_ge(s["x2"], n)
                    nc.tensor.matmul(bank[7][:, 0:D], onesb[:, :], bout, start=True, stop=False)
                    for c in range(C):
                        mm = nc.tensor.matmul(bank[7][:, 0:D], qT[:, c, t * P:(t + 1) * P], aw[:, t // 2, c, :],
                                              start=False, stop=(c == C - 1))
                    mm.then_inc(s["o_ps"], 1)

            def keys_values(s, g):
                pe.wait_ge(s["xnT"], C * (g + 1))
                for t in range(GT):
                    n = g * GT + t
                    if n >= 2:
                        pe.wait_ge(s["kv"], n - 1)
                        pe.wait_ge(s["ssq"], 2 * (n - 1))
                    nc.tensor.matmul(bank[2 + n % 2][:, :], onesb[:, :], bkv, start=True, stop=False)
                    for c in range(C):
                        mm = nc.tensor.matmul(bank[2 + n % 2][:, :], xnT[:, 0, c, t * P:(t + 1) * P],
                                              win[:, c, D:3 * D], start=False, stop=(c == C - 1))
                    mm.then_inc(s["kv_ps"], 1)

            def queries(s, g):
                for m in range(C):
                    if g >= 1:
                        pe.wait_ge(s["qT"], C * (g - 1) + m + 1)
                    for c in range(C):
                        mm = nc.tensor.matmul(bank[5 + m][:, :], win[:, c, m * P:(m + 1) * P], xnT[:, 0, c, :],
                                              start=(c == 0), stop=(c == C - 1))
                    mm.then_inc(s["q_ps"], 1)

            def attention(s, front):
                for g in range(NG + 1):
                    if g >= 1:
                        if g >= 2:
                            pe.wait_ge(front["logit"], g - 1)
                        mix(s, g - 1)
                        project(s, g - 1)
                    if g < NG:
                        pe.wait_ge(s["xn"], g + 1)
                        if g >= 2:
                            pe.wait_ge(front["xnT"], C * (g - 1))
                        elif g == 1:
                            pe.wait_ge(s["xnT"], C)
                        group_transposes(s, g, 0, 1)
                        keys_values(s, g)
                    if g >= 1:
                        pe.wait_ge(front["xn"], g)
                        pe.wait_ge(s["xnT"], C * min(g + 1, NG))
                        if g == NG:
                            pe.wait_ge(front["xnT"], C * (g - 1))
                        group_transposes(front, g - 1, 0, 2)
                    if g < NG:
                        queries(s, g)
                    if g >= 1:
                        pe.wait_ge(s["amix"], g)
                        router(front, g - 1, 4, 1)

            pe.wait_ge(const_in, 32)
            pe.wait_ge(pw_in, 16)
            ffn_front(ffn[0])
            pe.wait_ge(ones_set, 2)
            routing(ffn[0])
            tile_loop(ffn[0], True)
            pe.wait_ge(attw_in, 32)
            attention(att, ffn[1])
            routing(ffn[1])
            tile_loop(ffn[1], False)

        @block.vector
        def _(dve):
            done = [0]
            V = nc.vector

            def step(ins):
                done[0] += 1
                ins.then_inc(dve_step, 1)
                return done[0]

            def settled(n=None):
                dve.wait_ge(dve_step, done[0] if n is None else n)

            def aggregate(s, b):
                settled()
                for t in range(GT):
                    m = V.bn_aggr(mv[:, b, t, :], stats[:, b, t, :])
                    if t < GT - 1:
                        step(m)
                    else:
                        m.then_inc(s["var"], 1)

            def normalise(s, b, count, src, dst, signal):
                dve.wait_ge(s["std"], count)
                step(V.reciprocal(rstd[:, b, :], rstd[:, b, :]))
                dve.wait_ge(s["var"], count)
                settled()
                for t in range(GT):
                    m = V.tensor_scalar(dst(t), src(t), mv[:, b, t, 0:1], rstd[:, b, t:t + 1],
                                        ALU.subtract, ALU.mult)
                    if t == GT - 1:
                        m.then_inc(signal, 1)
                    else:
                        step(m)

            def top4(s, g, b):
                dve.wait_ge(s["logit_ps"], g + 1)
                V.tensor_tensor(logits[:, g * GT:(g + 1) * GT, :],
                                bank[b][:, 0:GT * EXPERTS].rearrange("p (t e) -> p t e", e=EXPERTS),
                                rb[:, :].unsqueeze(1).to_broadcast([P, GT, EXPERTS]),
                                ALU.add).then_inc(s["logit"], 1)
                dve.wait_ge(s["logit"], g + 1)
                for t in range(g * GT, (g + 1) * GT):
                    step(V.max(tops[:, t, :], logits[:, t, :]))
                settled()
                for t in range(g * GT, (g + 1) * GT):
                    step(V.max_index(topi[:, t, :], tops[:, t, :], logits[:, t, :]))

            def ffn_front(s):
                def stats_of(g):
                    dve.wait_ge(x_in[g], 16)
                    for t in range(GT):
                        step(V.bn_stats(stats[:, g % 2, t, :], X[:, g * GT + t, :]))
                    aggregate(s, g % 2)

                stats_of(0)
                for g in range(NG):
                    if g + 1 < NG:
                        stats_of(g + 1)
                    if g >= XBUF:
                        dve.wait_ge(s["xn_stored"][g % XBUF], 16 * (g // XBUF))
                        dve.wait_ge(s["xn_ps"], C * (g - XBUF + 1))
                    normalise(s, g % 2, g + 1, lambda t: X[:, g * GT + t, :], lambda t: xn[:, g % XBUF, t, :],
                              s["xn"])
                    if g >= 1:
                        top4(s, g - 1, 4 + (g - 1) % 2)
                top4(s, NG - 1, 4 + (NG - 1) % 2)

            def routing(s):
                settled()
                step(V.tensor_copy(topif[:, :, :], topi[:, :, 0:TOP_K]))
                V.tensor_tensor(wk[:, :, :], tops[:, :, 0:TOP_K],
                                tops[:, :, 0:1].to_broadcast([P, NT, TOP_K]), ALU.subtract).then_inc(s["wexp_in"], 1)
                settled()
                step(V.tensor_tensor(hot[:, :, :, :],
                                     const("iota").unsqueeze(1).unsqueeze(3)
                                     .to_broadcast([P, TOP_K, EXPERTS, NT]),
                                     topif.rearrange("p i k -> p k i").unsqueeze(2)
                                     .to_broadcast([P, TOP_K, EXPERTS, NT]), ALU.is_equal))
                settled()
                flat = hot.rearrange("p k e i -> p k (e i)")
                step(V.tensor_tensor(hot2, flat[:, 0:2, :], flat[:, 2:4, :], ALU.add))
                settled()
                step(V.tensor_tensor(mask, hot2[:, 0, :], hot2[:, 1, :], ALU.add))
                settled()
                V.tensor_tensor_scan(pre, const("seg"), mask, 0.0, ALU.mult, ALU.add).then_inc(s["pre"], 1)
                dve.wait_ge(s["wexp"], 1)
                step(V.tensor_reduce(wsum, wk[:, :, :], AX_X, ALU.add))
                settled()
                step(V.reciprocal(wrec, wsum))
                settled()
                step(V.scalar_tensor_tensor(wk[:, :, :], wk[:, :, :], 0.5,
                                            wrec.unsqueeze(2).to_broadcast([P, NT, TOP_K]), ALU.mult, ALU.mult))
                dve.wait_ge(s["cnt_ps"], 1)
                step(V.tensor_scalar(cnti, bank[6][:, EXPERTS * NT:EXPERTS * NT + EXPERTS], float(P - 1), None, ALU.add))
                settled()
                step(V.tensor_scalar(nt128, cnti, 7, 7, ALU.logical_shift_right, ALU.logical_shift_left))
                settled()
                step(V.tensor_tensor_scan(tend, onesb[:, 0:EXPERTS], nt128, 0.0, ALU.mult, ALU.add))
                settled()
                step(V.tensor_tensor(base, tend, nt128, ALU.subtract))
                settled()
                step(V.tensor_tensor(posall[:, :, :],
                                     bank[6][:, 0:EXPERTS * NT].rearrange("p (e i) -> p e i", e=EXPERTS),
                                     base.unsqueeze(2).to_broadcast([P, EXPERTS, NT]), ALU.add))
                settled()
                step(V.tensor_tensor(hotpos.rearrange("p k e i -> p k (e i)"), flat,
                                     posall.rearrange("p e i -> p (e i)").unsqueeze(1)
                                     .to_broadcast([P, TOP_K, EXPERTS * NT]), ALU.mult))
                step(V.tensor_scalar(ecmp, tend, const("part128"), None, ALU.is_le))
                settled()
                step(V.tensor_reduce(pos.rearrange("p (k i) -> p k i", k=TOP_K),
                                     hotpos.rearrange("p k e i -> p k i e"), AX_X, ALU.add))
                step(V.tensor_reduce(ecol, ecmp, AX_X, ALU.add))
                settled()
                step(V.tensor_copy(posi, pos))
                V.tensor_scalar(ecol, ecol, float(EXPERTS - 1), None, ALU.min).then_inc(s["ecol"], 1)
                settled()
                step(V.tensor_scalar(ji, posi, 7, None, ALU.logical_shift_right))
                settled()
                V.tensor_copy(jf, ji).then_inc(s["hot"], 1)
                dve.wait_ge(s["hot"], 1)
                step(V.scalar_tensor_tensor(sf, jf, -float(P), pos, ALU.mult, ALU.add))
                settled()
                for n in range(TOP_K * NT):
                    if n >= RING:
                        dve.wait_ge(s["place_ps"], n - RING + 1)
                    if n % 3 != 2:
                        V.tensor_scalar(tile_hot[:, n % RING, :], iota16[:, 0:TILES], jf[:, n:n + 1],
                                        const("tid1")[:, n % NT:n % NT + 1], ALU.is_equal,
                                        ALU.mult).then_inc(s["tile_hot"], 1)
                    V.tensor_scalar(slot_hot[:, n % RING, :], iota16, sf[:, n:n + 1], None,
                                    ALU.is_equal).then_inc(s["slot_hot"], 1)
                dve.wait_ge(s["etile_ps"], 1)
                V.tensor_copy(etile[0:1, :], bank[6][0:1, 0:P]).then_inc(s["etile"], 1)
                dve.wait_ge(s["place_ps"], TOP_K * NT)
                step(V.tensor_copy(codes[:, :, :], bank[7][:, 0:TOP_K * TILES].rearrange("p (k j) -> p k j", k=TOP_K)))
                settled()
                step(V.tensor_reduce(csum, codes.rearrange("p k j -> p j k"), AX_X, ALU.add))
                settled()
                V.tensor_scalar(gidx[:, :], csum, -1.0, 0.0, ALU.add, ALU.max).then_inc(s["gidx"], 1)
                step(V.tensor_scalar(ksum, codes[:, 1, :], 0.0, float(TOKENS), ALU.is_gt, ALU.mult))
                step(V.scalar_tensor_tensor(ppres, csum, 0.0, const("spare1"), ALU.is_equal, ALU.mult))
                for k in (2, 3):
                    step(V.tensor_scalar(codes[:, k, :], codes[:, k, :], 0.0, float(k * TOKENS), ALU.is_gt, ALU.mult))
                settled()
                step(V.tensor_tensor(ksum, ksum, codes[:, 2, :], ALU.add))
                step(V.tensor_tensor(ppres, ppres, csum, ALU.add))
                settled()
                step(V.tensor_tensor(ksum, ksum, codes[:, 3, :], ALU.add))
                settled()
                V.scalar_tensor_tensor(sidx[:, :], ksum, -1.0, ppres, ALU.add, ALU.add).then_inc(s["sidx"], 1)

            def tile(s, j, b, lo):
                gu = bank[2 + b]
                dve.wait_ge(s["gu_ps"], j + 1)
                if lo >= 2:
                    dve.wait_ge(s["sig"], j - 1)
                V.tensor_scalar(gate[:, b], gu[:, 0:HID], LIMIT, None, ALU.min).then_inc(s["gate"], 1)
                V.tensor_scalar(up[:, b], gu[:, HID:GU], LIMIT, -LIMIT, ALU.min, ALU.max).then_inc(s["gu_used"], 1)
                dve.wait_ge(s["gate"], j + 1)
                dve.wait_ge(s["gu_used"], j + 1)
                V.scalar_tensor_tensor(prod[:, b], up[:, b], 1.0, gate[:, b], ALU.add, ALU.mult).then_inc(s["prod"], 1)
                dve.wait_ge(s["prod"], j + 1)
                dve.wait_ge(s["sig"], j + 1)
                if lo >= 2:
                    dve.wait_ge(s["ht_ps"], j - 1)
                V.tensor_tensor(hid[:, b], prod[:, b], sig[:, b], ALU.mult).then_inc(s["hid"], 1)

            def tile_loop(s):
                for u in range(UNROLL):
                    tile(s, u, u % 2, u)
                with dve.Fori(UNROLL, TILES - UNROLL + 1, UNROLL) as j0:
                    for u in range(UNROLL):
                        tile(s, j0 + u, u % 2, 8)

            def combine(s, i, k, after, ring, buf):
                if k == 0:
                    dve.wait_ge(s["y_back"][i % ring], 16 * (i // ring + 1))
                else:
                    settled(after)
                m = V.scalar_tensor_tensor(X[:, i, :], buf[:, i % ring, k, :], wk[:, i, k:k + 1], X[:, i, :],
                                           ALU.mult, ALU.add)
                if k < TOP_K - 1:
                    return step(m)
                m.then_inc(s["combined"], 1)

            def combine_and_rotate(s, before, g, t):
                i, n = g * GT + t, (g - 1) * GT + t
                after = combine(before, i, 0, None, 2, yc) if g < NG else None
                if g >= 1:
                    dve.wait_ge(s["kv"], n + 1)
                    if n >= 1:
                        dve.wait_ge(s["kvprod"], n)
                    half = t % 2
                    cos = const("cos")[:, half * ROT:(half + 1) * ROT].unsqueeze(1).to_broadcast([P, 2, ROT])
                    k_and_v = kv[:, t, :].rearrange("p (m d) -> p m d", m=2)
                    at_rot = step(V.tensor_tensor(rot, k_and_v[:, :, 0:ROT], cos, ALU.mult))
                if g < NG:
                    after = combine(before, i, 1, after, 2, yc)
                if g >= 1:
                    sines = rots[:, n % 2, :].rearrange("p (m d) -> p m d", m=2)
                    dve.wait_ge(s["rots"], n + 1)
                    settled(at_rot)
                    step(V.tensor_tensor(rot[:, :, 0:HALF], rot[:, :, 0:HALF], sines[:, :, HALF:ROT], ALU.add))
                    at_rot = step(V.tensor_tensor(rot[:, :, HALF:ROT], rot[:, :, HALF:ROT], sines[:, :, 0:HALF],
                                                  ALU.add))
                if g < NG:
                    after = combine(before, i, 2, after, 2, yc)
                if g >= 1:
                    settled(at_rot)
                    if t == 0 and g >= 2:
                        dve.wait_ge(s["a_ps"], g - 1)
                    V.tensor_tensor(kvprod[:, t, 0:ROT], rot[:, 0, :], rot[:, 1, :],
                                    ALU.mult).then_inc(s["kvprod"], 1)
                if g < NG:
                    combine(before, i, 3, after, 2, yc)
                    dve.wait_ge(before["combined"], i + 1)
                    step(V.bn_stats(stats[:, 0, t, :], X[:, i, :]))

            def attention(s, before, front):
                for g in range(NG + 1):
                    if g >= 2:
                        top4(front, g - 2, 4)
                    for t in range(GT):
                        combine_and_rotate(s, before, g, t)
                    if g < NG:
                        aggregate(s, 0)
                    if g >= 1:
                        dve.wait_ge(s["norm"], g)
                        if g >= 2:
                            dve.wait_ge(s["a_ps"], g - 1)
                        step(V.tensor_tensor(rkv[:, :], nrm[:, :, 0], nrm[:, :, 1], ALU.mult))
                        settled()
                        V.reciprocal(rkv[:, :], rkv[:, :]).then_inc(s["rkv"], 1)
                    if g < NG:
                        if g >= 1:
                            dve.wait_ge(s["xsum"], GT * g)
                        normalise(s, 0, 2 * g + 1, lambda t: X[:, g * GT + t, :], lambda t: xn[:, 0, t, :], s["xin"])
                        dve.wait_ge(s["xin"], g + 1)
                        for t in range(GT):
                            step(V.bn_stats(stats[:, 1, t, :], xn[:, 0, t, :]))
                        aggregate(s, 1)
                    if g >= 1:
                        dve.wait_ge(s["a_ps"], g)
                        V.tensor_scalar(amix.rearrange("p b c -> p (b c)"), bank[4][:, 0:2 * C], 0.5, 0.5, ALU.mult,
                                        ALU.add).then_inc(s["amix"], 1)
                        dve.wait_ge(s["amix"], g)
                        if g >= 2:
                            dve.wait_ge(s["o_ps"], GT * (g - 1))
                        for b in range(2):
                            for c in range(C):
                                m = V.tensor_scalar(aw[:, b, c, :], wout[:, c, :], amix[:, b, c:c + 1], None, ALU.mult)
                                if c < C - 1:
                                    step(m)
                                else:
                                    m.then_inc(s["aw"], 1)
                    if g < NG:
                        if g >= 1:
                            dve.wait_ge(s["xn_ps"], C * g)
                        normalise(s, 1, 2 * g + 2, lambda t: xn[:, 0, t, :], lambda t: xn[:, 1, t, :], s["xn"])
                    if g >= 1:
                        dve.wait_ge(s["xsum"], GT * g)
                        for t in range(GT):
                            n = (g - 1) * GT + t
                            dve.wait_ge(s["o_ps"], n + 1)
                            V.tensor_tensor(X[:, n, :], bank[7][:, 0:D], X[:, n, :], ALU.add).then_inc(s["x2"], 1)
                            dve.wait_ge(s["x2"], n + 1)
                            step(V.bn_stats(stats[:, 2, t, :], X[:, n, :]))
                        aggregate(front, 2)
                        if g >= 2:
                            dve.wait_ge(front["xn_stored"][2], 16 * (g - 1))
                            dve.wait_ge(front["xn_ps"], C * (g - 1))
                        normalise(front, 2, g, lambda t: X[:, (g - 1) * GT + t, :], lambda t: xn[:, 2, t, :],
                                  front["xn"])
                top4(front, NG - 1, 4)

            dve.wait_ge(const_in, 32)
            dve.wait_ge(bias_in, 16)
            step(V.tensor_copy(bpart[:, 0, :], bsrc))
            settled()
            step(V.tensor_tensor(bres, bsrc, bpart[:, 0, :], ALU.subtract))
            settled()
            step(V.tensor_copy(bpart[:, 1, :], bres))
            settled()
            step(V.tensor_tensor(bres2, bres, bpart[:, 1, :], ALU.subtract))
            settled()
            V.tensor_copy(bpart[:, 2, :], bres2).then_inc(bias_split, 1)
            dve.wait_ge(bias_split, 1)
            dve.wait_ge(rbias_in, 16)
            dve.wait_ge(ones_set, 2)
            ffn_front(ffn[0])
            routing(ffn[0])
            tile_loop(ffn[0])
            dve.wait_ge(attw_in, 32)
            attention(att, ffn[0], ffn[1])
            routing(ffn[1])
            tile_loop(ffn[1])
            for i in range(0, NT, 2):
                after = [None, None]
                for k in range(TOP_K):
                    for h in range(2):
                        after[h] = combine(ffn[1], i + h, k, after[h], YL, yl)


def _constants():
    p = np.arange(P)
    c = np.zeros((P, CONST_W), np.float32)

    def put(name, v):
        at, w = CONST[name]
        c[:, at:at + w] = np.asarray(v, np.float32).reshape(-1, w) if np.ndim(v) else v

    put("ident", np.eye(P))
    put("iota", np.tile(np.arange(EXPERTS), (P, 1)))
    put("seg", np.tile((np.arange(EXPERTS * NT) % NT != 0), (P, 1)))
    put("tid1", np.arange(NT)[None, :] * P + p[:, None] + 1)
    put("part128", p[:, None] * P)
    put("spare1", TOP_K * TOKENS + np.arange(TILES)[None, :] * P + p[:, None] + 1)
    inv = (1.0 / 10000.0 ** (np.arange(0, ROT, 2, dtype=np.float32) / np.float32(ROT))).astype(np.float32)
    ang = (np.arange(SEQ, dtype=np.float32)[:, None] * inv[None, :]).astype(np.float32)
    cos, sin = np.cos(ang), np.sin(ang)
    put("cos", np.concatenate([np.concatenate([cos[h * P:(h + 1) * P]] * 2, 1) for h in range(2)], 1))
    put("sin", np.concatenate([np.concatenate([sin[h * P:(h + 1) * P], -sin[h * P:(h + 1) * P]], 1) for h in range(2)], 1))
    c16 = np.concatenate([(p[:, None] < p[None, :]) - 1.0, np.tile(p, (P, 1))], 1).astype(np.float16)
    return c, c16


def kernel(**inputs):
    import concourse.bacc as _bacc
    from concourse.bass_utils import run_bass_kernel_spmd as _run

    a = {k[3:]: np.asarray(v) for k, v in inputs.items()}
    perm = np.concatenate([np.arange(0, ROT, 2), np.arange(1, ROT, 2), np.arange(ROT, D)])
    perm3 = np.concatenate([perm, D + perm, 2 * D + perm])

    def chunks(w):
        return w.reshape(C, P, -1).transpose(1, 0, 2)

    w_in = chunks(a["attn_W_in"][:, perm3])
    w_out = chunks(a["attn_W_out"][perm, :])
    b_in = a["attn_b_in"][perm3]
    w_gu = a["ffn_gate_up_proj"].reshape(EXPERTS, C, P, HID, 2).transpose(2, 0, 1, 4, 3).reshape(P, EXPERTS, C, GU)
    w_dn = a["ffn_down_proj"].reshape(EXPERTS, C, P, D).transpose(2, 0, 1, 3)
    b_gu = a["ffn_gate_up_proj_bias"].reshape(EXPERTS, HID, 2).transpose(0, 2, 1).reshape(EXPERTS, GU)
    bias = np.concatenate([np.concatenate([b_gu, a["ffn_down_proj_bias"]], 1).ravel(), b_in[D:],
                           a["attn_b_out"]]).reshape(P, BCOL)
    pweights = np.concatenate([
        chunks(a["ffn_router_weight"].T).reshape(P, -1), a["attn_gamma"].reshape(C, P).T,
        a["attn_beta"].reshape(C, P).T, b_in[:D].reshape(C, P).T], 1)
    consts, consts16 = _constants()
    sent = {"x": a["attn_X"].reshape(TOKENS, D), "consts": consts, "consts16": consts16, "rbias": a["ffn_router_bias"], "pweights": pweights,
            "w_in": w_in, "w_out": w_out, "w_gu": w_gu, "w_down": w_dn, "bias": bias}
    nc = _bacc.Bacc("TRN2", target_bir_lowering=False, num_devices=1)
    arrays, args = {}, []
    for name, v in sent.items():
        v = np.ascontiguousarray(v)
        arrays[f"in_{name}"] = v
        args.append(nc.dram_tensor(f"in_{name}", v.shape, mybir.dt.from_np(v.dtype), kind="ExternalInput").ap())
    args.append(nc.dram_tensor("out", [TOKENS, D], F32, kind="ExternalOutput").ap())
    macaron_kernel(nc, *args)
    r = _run(nc, [arrays], core_ids=[0])
    return r.results[0]["out"].reshape(BATCH, SEQ, D)
```

```python
from contextlib import ExitStack

import numpy as np
import concourse.bass as bass
from concourse import mybir

ALU = mybir.AluOpType
ACT = mybir.ActivationFunctionType
F32 = mybir.dt.float32
F16 = mybir.dt.float16
BF16 = mybir.dt.bfloat16
I32 = mybir.dt.int32
U32 = mybir.dt.uint32
AX_X = mybir.AxisListType.X

P = 128
BATCH, SEQ, D = 8, 256, 256
TOKENS = BATCH * SEQ
NT = TOKENS // P
GT = 4
NG = NT // GT
C = D // P
EXPERTS, TOP_K = 16, 4
HID = 256
GU = 2 * HID
UNROLL = 4
YC = 3
YL = 4
LATE = 2
TILES = TOKENS * TOP_K // P + EXPERTS - 1
LONG = 2 * UNROLL
TILES = -(-TILES // LONG) * LONG
ROT = D // 2
HALF = ROT // 2
LIMIT, ALPHA = 7.0, 1.702
EPS = 1e-5
BW = GU + D
OUT_BANKS = (7, 5, 6, 7)
BROWS = 3 * (EXPERTS + 1)
BCOL = (EXPERTS + 1) * BW // P
WE = C * GU + C * D
WB = EXPERTS // NG
GRAMS = WB * WE // P
BATCH2_AT = 6
GRAMS_AT = 8
SUMS_AT = GRAMS_AT + GRAMS // 4
LO_AT = SUMS_AT + 3
BEFORE_STORES = (4, 7, 10, 13)
POOL_E = [WB - 1] * (NG - 1) + [WB]
POOL_ALL = sum(POOL_E)
STEP_E = 2
H_SCALE = 256.0
XBUF = 3

CONST = {}
for _n, _w in (("ident", P), ("iota", EXPERTS), ("seg", EXPERTS * NT), ("tid1", NT), ("part128", 1),
               ("emask", EXPERTS + 1), ("spare1", TILES), ("cos", 2 * ROT), ("sin", 2 * ROT)):
    CONST[_n] = (sum(w for _, w in CONST.values()), _w)
CONST_W = sum(w for _, w in CONST.values())
PW = {"rw": (0, C * EXPERTS), "gamma": (C * EXPERTS, C), "beta": (C * EXPERTS + C, C), "bq": (C * EXPERTS + 2 * C, C)}
PW_W = C * EXPERTS + 3 * C
T_LIM, T_NLIM, T_S, T_ALPHA, T_HID, T_Y, T_W = range(7)


def macaron_kernel(nc, x, consts, consts16, rbias, pweights, w_in, w_out, w_exp, bias, out):
    x_v = x.rearrange("(i p) d -> p i d", p=P)
    out_v = out.rearrange("(i p) d -> p i d", p=P)
    xn_dram = nc.dram_tensor("xn_dram", [TOKENS, 2 * D], F16, kind="Internal").ap()
    y_dram = nc.dram_tensor("y_dram", [TOP_K * TOKENS + TILES * P, D], F32, kind="Internal").ap()
    y_v = y_dram[0:TOP_K * TOKENS, :].rearrange("(k i p) d -> p k i d", k=TOP_K, p=P)
    bias_dram = [nc.dram_tensor(f"bias_dram{w}", [3, (EXPERTS + 1) * w], BF16, kind="Internal").ap()
                 for w in (GU, D)]
    xn_v = xn_dram.rearrange("(i p) d -> p i d", p=P)

    with ExitStack() as ctx:
        def sb(name, shape, dt=F32):
            return ctx.enter_context(nc.sbuf_tensor(name, shape, dt))

        def sem(name):
            return ctx.enter_context(nc.semaphore(name))

        bank = [ctx.enter_context(nc.psum_tensor(f"bank{n}", [P, 512], F32)) for n in range(8)]

        wexp = sb("wexp", [P, EXPERTS, WE])
        w16 = wexp[:, :, :].bitcast(F16)
        biases = sb("biases", [P, BW], BF16)
        pick = sb("pick", [P, EXPERTS + 2], BF16)
        bkv, bout = biases[:, 0:2 * D], biases[:, 2 * D:BW]
        X = sb("X", [P, NT, D])
        xnT = sb("xnT", [P, 2, C, GT * P])
        win = sb("win", [P, C, 3 * D])
        wout = sb("wout", [P, C, D])
        cst = sb("cst", [P, CONST_W])
        rb = sb("rb", [P, EXPERTS])
        pw = sb("pw", [P, PW_W])
        xn = sb("xn", [P, XBUF, GT, D])
        xs = sb("xs", [P, 2, GT, 2 * D], F16)
        onesb = sb("onesb", [P, P], BF16)
        cst16 = sb("cst16", [P, 3 * P], F16)
        lowm, iota16, ident16 = cst16[:, 0:P], cst16[:, P:2 * P], cst16[:, 2 * P:3 * P]
        wdiag = sb("wdiag", [P, WB, P])
        wsq = sb("wsq", [P, EXPERTS])
        wtot = sb("wtot", [P, EXPERTS])
        wint = sb("wint", [P, 3, EXPERTS], I32)
        wscale = sb("wscale", [P, EXPERTS])
        winv = sb("winv", [P, EXPERTS])
        table = sb("table", [P, EXPERTS, T_W])
        cols = sb("cols", [P, 4, T_W])
        epsc = sb("epsc", [P, 1])
        stats = sb("stats", [P, 3, GT, 6])
        mv = sb("mv", [P, 3, GT, 2])
        rstd = sb("rstd", [P, 3, GT])
        tops = sb("tops", [P, NT, 8])
        wk = sb("wk", [P, NT, TOP_K])
        gidx = sb("gidx", [P, TILES], U32)
        sidx = sb("sidx", [P, TILES], U32)
        etile = sb("etile", [1, P], I32)
        gcol = sb("gcol", [P, UNROLL], U32)
        scol = sb("scol", [P, UNROLL], U32)
        WORK = 24 * 256
        work = sb("work", [P, WORK])

        def wk_area(at, *shape):
            n = int(np.prod(shape))
            names = "abc"[:len(shape)]
            v = work[:, at:at + n]
            if len(shape) == 1:
                return v
            return v.rearrange(f"p ({' '.join(names)}) -> p {' '.join(names)}",
                               **{names[i]: shape[i] for i in range(len(shape))})

        xg = wk_area(0, 4 * D).bitcast(F16).rearrange("p (u d) -> p u d", u=4)
        yb = wk_area(4 * D, 4, D)
        xT = wk_area(8 * D, 2 * D).bitcast(F16).rearrange("p (b h c n) -> p b h c n", b=2, h=2, c=C)
        hT = wk_area(10 * D, 2 * D).bitcast(F16).rearrange("p (b h c n) -> p b h c n", b=2, h=2, c=C)
        gate = wk_area(12 * D, 2, D)
        up = wk_area(14 * D, 2, D)
        prod = wk_area(16 * D, 2, D)
        sig = wk_area(18 * D, 2, D)
        hid = wk_area(20 * D, 2, D)
        yc = sb("yc", [P, YC, TOP_K, D])
        yl = wk_area(0, YL, TOP_K, D)
        logits = sb("logits", [P, NT, EXPERTS])
        topi = sb("topi", [P, NT, 8], U32)
        topif = wk_area(256, NT, TOP_K)
        hot = wk_area(512, TOP_K, EXPERTS, NT)
        hot2 = wk_area(1536, 2, EXPERTS * NT)
        mask = wk_area(2048, EXPERTS * NT // 2).bitcast(F16)
        pre = wk_area(2304, EXPERTS * NT // 2).bitcast(F16)
        posall = wk_area(2560, EXPERTS, NT)
        hotpos = wk_area(2816, TOP_K, EXPERTS, NT)
        pos = wk_area(3840, TOP_K * NT)
        jf = wk_area(3904, TOP_K * NT)
        sf = wk_area(3968, TOP_K * NT)
        posi = wk_area(4032, TOP_K * NT).bitcast(I32)
        ji = wk_area(4096, TOP_K * NT).bitcast(I32)
        cnti = wk_area(4160, EXPERTS).bitcast(I32)
        nt128 = wk_area(4176, EXPERTS).bitcast(I32)
        tend = wk_area(4192, EXPERTS)
        base = wk_area(4208, EXPERTS)
        ecmp = wk_area(4224, EXPERTS)
        ecol = wk_area(4240, 1)
        wsum = wk_area(448, NT)
        wrec = wk_area(464, NT)
        codes = wk_area(4244, TOP_K, TILES)
        csum = wk_area(4564, TILES)
        ksum = wk_area(4644, TILES)
        ppres = wk_area(4724, TILES)
        RING = 8
        slot_hot = wk_area(4804, RING * P // 2).bitcast(F16).rearrange("p (r s) -> p r s", r=RING)
        tile_hot = wk_area(4804 + RING * P // 2, RING * TILES // 2).bitcast(F16).rearrange("p (r s) -> p r s", r=RING)
        kv = wk_area(2048, GT, 2 * D)
        rot = wk_area(4096, 2, ROT)
        rots = wk_area(4352, 2, 2 * ROT)
        kvprod = wk_area(4864, GT, D)
        junk = wk_area(5888, D)
        att_buf = sb("att_buf", [P, 2 * C * D + C * GT * P])
        aw = att_buf[:, 0:2 * C * D].rearrange("p (b c d) -> p b c d", b=2, c=C)
        qT = att_buf[:, 2 * C * D:].rearrange("p (c n) -> p c n", c=C)
        raw_places = [wexp[:, e + STEP_E, :] for e in range(EXPERTS - STEP_E)]
        raw_places += [att_buf[:, 0:WE], win[:, :, :].rearrange("p c n -> p (c n)")]
        ones32 = wk_area(0, P)
        ssq = sb("ssq", [P, GT, 2])
        nrm = sb("nrm", [P, GT, 2])
        rkv = sb("rkv", [P, GT])
        amix = sb("amix", [P, 2, C])
        BIAS_AT = WORK - 9 * BCOL // 2
        bsrc = wk_area(BIAS_AT, BCOL)
        bres = wk_area(BIAS_AT + BCOL, BCOL)
        bres2 = wk_area(BIAS_AT + 2 * BCOL, BCOL)
        bpart = wk_area(BIAS_AT + 3 * BCOL, 3 * BCOL // 2).bitcast(BF16).rearrange("p (n j) -> p n j", n=3)

        def const(name):
            at, w = CONST[name]
            return cst[:, at:at + w]

        def experts_into_registers(numbers, engine):
            _, values = nc.values_load_multi_w_load_instructions(
                numbers, engines=[engine], min_val=0, max_val=EXPERTS - 1,
                skip_runtime_bounds_check_because="the routing bounds them by EXPERTS - 1")
            return values

        def sums_bank(g):
            return bank[7] if g < 2 else bank[g - 2]

        def turned(b):
            return bank[b][:, 0:D].bitcast(F16)

        def pwt(name):
            at, w = PW[name]
            return pw[:, at:at + w]

        rw = pwt("rw").rearrange("p (c e) -> p c e", c=C)

        const_in, pw_in, attw_in = map(
            sem, ("const_in", "pw_in", "attw_in"))
        w_loaded = [sem(f"w_loaded{b}") for b in range(NG)]
        table_set, bias_split, bias_stored, bias_rows, ones_set = map(
            sem, ("table_set", "bias_split", "bias_stored", "bias_rows", "ones_set"))
        w_grams, w_diag, w_sums, w_scales, w_hi, w_scaled, w_lo, w_lo_dve = map(
            sem, ("w_grams", "w_diag", "w_sums", "w_scales", "w_hi", "w_scaled", "w_lo", "w_lo_dve"))
        x_in = [sem(f"x_in{g}") for g in range(NG)]
        dve_step = sem("dve_step")
        out_stored = sem("out_stored")

        def signals(tag, names, **lists):
            one = {n: sem(f"{tag}_{n}") for n in names.split()}
            one.update({n: [sem(f"{tag}_{n}{m}") for m in range(count)] for n, count in lists.items()})
            return one

        FFN = ("var std xn xn_ps xnT logit_ps logit wexp_in wexp pre cnt_ps hot slot_hot tile_hot place_ps cols gcol scol "
               "ecol etile_ps etile gidx sidx xhi xlo xt_ps xt tcols gu_ps gate up prod sig hid ht_ps hid_hi hid_lo y_ps y")
        ffn = [signals(f"ffn{f}", FFN + (" combined", " combined tile_hot_pool")[f], xn_stored=2, gathered=UNROLL,
                       scattered=UNROLL, y_back=(YC, YL)[f])
               for f in range(2)]
        att = signals("att", "var std xin xn xn_ps xnT kv_ps kv ssq norm rots xsum kvpass kvprod rkv a_ps amix aw q_ps qT "
                             "o_ps x2")

        block = ctx.enter_context(nc.Block())

        @block.sync
        def _(sp):
            sp.dma_start(cst[:, :], consts).then_inc(const_in, 16)
            sp.dma_start(cst16[:, :], consts16).then_inc(const_in, 16)
            for g in range(NG):
                sp.dma_start(X[:, g * GT:(g + 1) * GT, :], x_v[:, g * GT:(g + 1) * GT, :]).then_inc(x_in[g], 16)
            sp.dma_start(pw[:, :], pweights).then_inc(pw_in, 16)
            sp.dma_start(rb[:, :], rbias.partition_broadcast(P)).then_inc(pw_in, 16)
            sp.dma_start(bsrc, bias).then_inc(pw_in, 16)
            for e in range(EXPERTS):
                sp.dma_start(raw_places[e], w_exp[:, e, :]).then_inc(w_loaded[e // WB], 16)
                if e in BEFORE_STORES:
                    g = BEFORE_STORES.index(e)
                    sp.wait_ge(ffn[0]["xn_stored"][g % 2], 16 * (g // 2 + 1))
            sp.wait_ge(w_hi, EXPERTS)
            sp.wait_ge(w_lo, POOL_ALL)
            sp.dma_start(win[:, :, :], w_in).then_inc(attw_in, 16)
            sp.dma_start(wout[:, :, :], w_out).then_inc(attw_in, 16)
            for f in range(2):
                ring, buf = ((YC, yc), (YL, yl))[f]
                for u in range(UNROLL):
                    sp.wait_ge(ffn[f]["scattered"][u], 16 * TILES // UNROLL)
                for i in range(NT):
                    if i >= ring:
                        sp.wait_ge(ffn[f]["combined"], i - ring + 1)
                    sp.dma_start(buf[:, i % ring], y_v[:, :, i, :]).then_inc(ffn[f]["y_back"][i % ring], 16)
            for i in range(NT):
                sp.wait_ge(ffn[1]["combined"], i + 1)
                sp.dma_start(out_v[:, i, :], X[:, i, :]).then_inc(out_stored, 16)
            sp.wait_ge(out_stored, 16 * NT)

        @block.gpsimd
        def _(pool):
            nc.gpsimd.memset(onesb[:, :], 1.0).then_inc(ones_set, 1)
            nc.gpsimd.memset(epsc[:, :], EPS).then_inc(ones_set, 1)
            nc.gpsimd.memset(ones32, 1.0).then_inc(ones_set, 1)
            nc.gpsimd.memset(biases[:, :], 0.0).then_inc(ones_set, 1)

            def split_lo(s, g, xb):
                pool.wait_ge(s["xhi"], g + 1)
                nc.gpsimd.tensor_tensor(xs[:, g % 2, :, D:2 * D], xn[:, xb], xs[:, g % 2, :, 0:D],
                                        ALU.subtract).then_inc(s["xlo"], 1)

            def weights_lo(g):
                for e in range(g * WB, g * WB + POOL_E[g]):
                    pool.wait_ge(w_scaled, sum(POOL_E[:g]) + e % WB + 1)
                    nc.gpsimd.tensor_tensor(w16[:, e, WE:2 * WE], raw_places[e], w16[:, e, 0:WE],
                                            ALU.subtract).then_inc(w_lo, 1)

            def tile_hots(s):
                pool.wait_ge(const_in, 32)
                pool.wait_ge(s["hot"], 1)
                for n in range(2, TOP_K * NT, 3):
                    if n >= RING:
                        pool.wait_ge(s["place_ps"], n - RING + 1)
                    nc.gpsimd.tensor_scalar(tile_hot[:, n % RING, :], iota16[:, 0:TILES], jf[:, n:n + 1],
                                            const("tid1")[:, n % NT:n % NT + 1], ALU.is_equal,
                                            ALU.mult).then_inc(s["tile_hot_pool"], 1)

            def tile(s, j, u, lo):
                if lo + UNROLL < TILES:
                    pool.wait_ge(s["xt_ps"], j + 1)
                    gather(s, j + UNROLL, u)
                if lo >= LATE:
                    scatter(s, j - LATE, (u - LATE) % UNROLL, lo - LATE)

            def copy_cols(s, dst, src, signal, count):
                nc.gpsimd.tensor_copy(dst, src).then_inc(signal, 1)
                pool.wait_ge(signal, count)
                pool.sem_inc(s["cols"], 1)

            def gather(s, j, u):
                copy_cols(s, gcol[:, u:u + 1], gidx[:, bass.ds(j, 1)], s["gcol"], j + 1)
                nc.gpsimd.indirect_dma_start(
                    out=xg[:, u, :], out_offset=None, in_=xn_dram,
                    in_offset=bass.IndirectOffsetOnAxis(ap=gcol[:, u:u + 1], axis=0)).then_inc(s["gathered"][u], 16)

            def scatter(s, j, u, lo):
                if lo >= UNROLL:
                    pool.wait_ge(s["scattered"][u], 4 * j - 4 * u)
                pool.wait_ge(s["y"], j + 1)
                copy_cols(s, scol[:, u:u + 1], sidx[:, bass.ds(j, 1)], s["scol"], j + 1)
                nc.gpsimd.indirect_dma_start(
                    out=y_dram, out_offset=bass.IndirectOffsetOnAxis(ap=scol[:, u:u + 1], axis=0),
                    in_=yb[:, u, :], in_offset=None).then_inc(s["scattered"][u], 16)

            def bias_parts_to_rows():
                pool.wait_ge(bias_split, 1)
                sides = ((0, GU), (GU, D))
                for dram, (at, w) in zip(bias_dram, sides):
                    nc.gpsimd.dma_start(dram.rearrange("n (p j) -> p n j", p=P),
                                        bpart[:, :, BCOL * at // BW:BCOL * (at + w) // BW]).then_inc(bias_stored, 16)
                pool.wait_ge(bias_stored, 32)
                pool.wait_ge(ones_set, 4)
                for dram, (at, w) in zip(bias_dram, sides):
                    nc.gpsimd.dma_start(biases[0:BROWS, at:at + w],
                                        dram.rearrange("n (e w) -> (n e) w", w=w)).then_inc(bias_rows, 16)

            def attention(s, front):
                for g in range(NG + 1):
                    for t in range(GT):
                        n = (g - 1) * GT + t
                        if g == 0:
                            continue
                        half = t % 2
                        pool.wait_ge(s["kv"], n + 1)
                        if n >= 2:
                            pool.wait_ge(s["kvprod"], n - 1)
                        k_and_v = kv[:, t, :].rearrange("p (m d) -> p m d", m=2)
                        sin = const("sin")[:, half * ROT:(half + 1) * ROT].unsqueeze(1).to_broadcast([P, 2, ROT])
                        nc.gpsimd.tensor_tensor(rots[:, n % 2, :].rearrange("p (m d) -> p m d", m=2),
                                                k_and_v[:, :, 0:ROT], sin, ALU.mult).then_inc(s["rots"], 1)
                        if t == 0 and g >= 2:
                            pool.wait_ge(s["a_ps"], g - 1)
                        nc.gpsimd.tensor_tensor(kvprod[:, t, ROT:D], k_and_v[:, 0, ROT:D], k_and_v[:, 1, ROT:D],
                                                ALU.mult).then_inc(s["kvpass"], 1)
                    if g >= 2:
                        split_lo(front, g - 2, 2)
                    if g < NG:
                        pool.wait_ge(s["xin"], g + 1)
                        for t in range(GT):
                            n = g * GT + t
                            nc.gpsimd.tensor_tensor(X[:, n, :], X[:, n, :], xn[:, 0, t, :],
                                                    ALU.add).then_inc(s["xsum"], 1)

                split_lo(front, NG - 1, 2)

            for f in range(2):
                s = ffn[f]
                if f == 1:
                    attention(att, s)
                    tile_hots(s)
                else:
                    split_lo(s, 0, 0)
                    bias_parts_to_rows()
                    for g in range(1, NG):
                        split_lo(s, g, g % XBUF)
                    for g in range(NG):
                        weights_lo(g)
                pool.wait_ge(s["gidx"], 1)
                for b in range(2):
                    pool.wait_ge(s["xn_stored"][b], 16 * NG // 2)
                for u in range(UNROLL):
                    gather(s, u, u)
                pool.wait_ge(s["sidx"], 1)
                for u in range(2 * UNROLL):
                    tile(s, u, u % UNROLL, u)
                with pool.Fori(2 * UNROLL, TILES - 2 * UNROLL + 1, UNROLL) as j0:
                    for u in range(UNROLL):
                        tile(s, j0 + u, u, 2 * UNROLL)
                for u in range(UNROLL):
                    tile(s, TILES - UNROLL + u, u, TILES - UNROLL + u)
                for j in range(TILES - LATE, TILES):
                    scatter(s, j, j % UNROLL, j)

        @block.scalar
        def _(act):
            act.wait_ge(ones_set, 3)

            def std_of(s, count, b):
                act.wait_ge(s["var"], count)
                nc.scalar.activation(rstd[:, b, :], mv[:, b, :, 1], ACT.Sqrt, bias=epsc[:, 0:1]).then_inc(s["std"], 1)

            def split_hi(s, g, xb):
                act.wait_ge(s["xn"], g + 1)
                if g >= 2:
                    act.wait_ge(s["xn_stored"][g % 2], 16 * (g // 2))
                nc.scalar.activation(xs[:, g % 2, :, 0:D], xn[:, xb], ACT.Copy).then_inc(s["xhi"], 1)

            def store_xn(s, g):
                act.wait_ge(s["xlo"], g + 1)
                nc.scalar.dma_start(xn_v[:, g * GT:(g + 1) * GT, :], xs[:, g % 2]).then_inc(s["xn_stored"][g % 2], 16)

            def weights_hi(g):
                act.wait_ge(w_scales, g + 1)
                for e in range(g * WB, (g + 1) * WB):
                    b, n = divmod(e - STEP_E, WB)
                    if e >= STEP_E and n < POOL_E[b]:
                        act.wait_ge(w_lo, sum(POOL_E[:b]) + n + 1)
                    elif e >= STEP_E:
                        act.wait_ge(w_lo_dve, b + 1)
                    nc.scalar.activation(w16[:, e, 0:WE], raw_places[e], ACT.Copy,
                                         scale=wscale[:, e:e + 1]).then_inc(w_hi, 1)
                    if e % WB < POOL_E[g]:
                        act.wait_ge(w_hi, e + 1)
                        nc.scalar.activation(raw_places[e], raw_places[e], ACT.Copy,
                                             scale=wscale[:, e:e + 1]).then_inc(w_scaled, 1)

            def take_xnT(s, g, b, tb):
                for c in range(C):
                    act.wait_ge(s["xn_ps"], C * g + c + 1)
                    nc.scalar.activation(xnT[:, tb, c, :], bank[b + c][:, :], ACT.Copy).then_inc(s["xnT"], 1)

            def ffn_front(s):
                std_of(s, 1, 0)
                for g in range(NG):
                    if g + 1 < NG:
                        std_of(s, g + 2, (g + 1) % 2)
                    split_hi(s, g, g % XBUF)
                    if g >= 2:
                        act.wait_ge(s["logit_ps"], g - 1)
                    take_xnT(s, g, C * (g % 2), g % 2)
                    store_xn(s, g)
                for g in range(NG):
                    if g == 2:
                        weights_exp(s)
                    weights_hi(g)

            def weights_exp(s):
                act.wait_ge(s["wexp_in"], 1)
                nc.scalar.activation(wk[:, :, :], wk[:, :, :], ACT.Exp).then_inc(s["wexp"], 1)

            def tile(s, j, u, nxt, prv, prv2, lo, e):
                b = u % 2
                if nxt:
                    take_xt(s, j + 1, (u + 1) % UNROLL, lo + 1, e)
                if prv:
                    hidden_hi(s, j - 1, (u + 1) % 2, lo - 1)
                act.wait_ge(s["gate"], j + 1)
                if lo >= 2:
                    act.wait_ge(s["hid"], j - 1)
                nc.scalar.activation(sig[:, b], gate[:, b], ACT.Sigmoid,
                                     scale=cols[:, u % UNROLL, T_ALPHA:T_ALPHA + 1]).then_inc(s["sig"], 1)
                if prv2:
                    take_y(s, j - 2, (u + 2) % UNROLL, lo - 2)

            def take_xt(s, j, u, lo, e):
                act.wait_ge(s["xt_ps"], j + 1)
                if lo >= 2:
                    act.wait_ge(s["gu_ps"], j - 1)
                nc.scalar.activation(xT[:, u % 2].rearrange("p h c n -> p (h c n)"), turned(u % 2),
                                     ACT.Copy).then_inc(s["xt"], 1)
                if lo >= 4:
                    act.wait_ge(s["hid"], j - 3)
                    act.wait_ge(s["y"], j - 3)
                nc.scalar.activation(cols[:, u, :], table[:, bass.ds(e, 1), :].rearrange("p o n -> p (o n)"),
                                     ACT.Copy).then_inc(s["tcols"], 1)

            def hidden_hi(s, j, b, lo):
                act.wait_ge(s["ht_ps"], j + 1)
                if lo >= 2:
                    act.wait_ge(s["y_ps"], j - 1)
                nc.scalar.activation(hT[:, b, 0].rearrange("p c n -> p (c n)"), bank[4 + b][:, 0:D],
                                     ACT.Copy).then_inc(s["hid_hi"], 1)

            def take_y(s, j, u, lo):
                act.wait_ge(s["y_ps"], j + 1)
                act.wait_ge(s["tcols"], j + 1)
                if lo >= 4:
                    act.wait_ge(s["scattered"][u], 4 * j - 4 * u)
                nc.scalar.activation(yb[:, u], bank[6 + u % 2][:, 0:D], ACT.Copy,
                                     scale=cols[:, u, T_Y:T_Y + 1]).then_inc(s["y"], 1)

            def tile_loop(s):
                act.wait_ge(s["etile"], 1)
                act.wait_ge(table_set, 1)
                def experts_of(j, count):
                    return experts_into_registers(etile[0:1, bass.ds(j, count)], mybir.EngineType.Activation)

                e = experts_of(0, LONG + 1)
                take_xt(s, 0, 0, 0, e[0])
                for u in range(LONG):
                    tile(s, u, u, True, u >= 1, u >= 2, u, e[u + 1])
                with act.Fori(LONG, TILES - 2 * LONG + 1, LONG) as j0:
                    e = experts_of(j0 + 1, LONG)
                    for u in range(LONG):
                        tile(s, j0 + u, u, True, True, True, LONG, e[u])
                e = experts_of(TILES - LONG, LONG)
                for u in range(LONG):
                    j = TILES - LONG + u
                    tile(s, j, u, u < LONG - 1, True, True, j, e[u + 1] if u < LONG - 1 else None)
                hidden_hi(s, TILES - 1, 1, TILES - 1)
                take_y(s, TILES - 2, 2, TILES - 2)
                take_y(s, TILES - 1, 3, TILES - 1)

            def take_kv(s, g, t):
                n = g * GT + t
                act.wait_ge(s["kv_ps"], n + 1)
                if g >= 1:
                    act.wait_ge(s["kvprod"], GT * g)
                    act.wait_ge(s["kvpass"], GT * g)
                nc.scalar.activation(kv[:, t, :], bank[2 + n % 2][:, :], ACT.Copy).then_inc(s["kv"], 1)
                if t == 0 and g >= 1:
                    act.wait_ge(s["norm"], g)
                for m in range(2):
                    if n or m:
                        act.wait_ge(s["ssq"], 2 * n + m)
                    nc.scalar.activation(junk, bank[2 + n % 2][:, m * D:(m + 1) * D], ACT.Square,
                                         accum_out=ssq[:, t, m:m + 1]).then_inc(s["ssq"], 1)

            def mix_weights(s, g):
                act.wait_ge(s["amix"], g)
                if g >= 2:
                    act.wait_ge(s["o_ps"], GT * (g - 1))
                for b in range(2):
                    for c in range(C):
                        m = nc.scalar.activation(aw[:, b, c, :], wout[:, c, :], ACT.Copy, scale=amix[:, b, c:c + 1])
                    m.then_inc(s["aw"], 1)

            def attention(s, front):
                for g in range(NG + 1):
                    if g < NG:
                        std_of(s, 2 * g + 1, 0)
                        std_of(s, 2 * g + 2, 1)
                    if g >= 1:
                        mix_weights(s, g)
                    if g < NG:
                        if g >= 1:
                            act.wait_ge(s["q_ps"], C * g)
                        for c in range(C):
                            act.wait_ge(s["xn_ps"], C * g + c + 1)
                            nc.scalar.activation(xnT[:, 0, c, :], bank[c][:, :], ACT.Identity,
                                                 bias=pwt("beta")[:, c:c + 1],
                                                 scale=pwt("gamma")[:, c:c + 1]).then_inc(s["xnT"], 1)
                        if g >= 1:
                            std_of(front, g, 2)
                        for t in range(GT):
                            take_kv(s, g, t)
                    else:
                        std_of(front, g, 2)
                    if g >= 2:
                        store_xn(front, g - 2)
                    if g >= 1:
                        split_hi(front, g - 1, 2)
                        if g >= 2:
                            act.wait_ge(front["logit_ps"], g - 1)
                        take_xnT(front, g - 1, 0, 1)
                    if g < NG:
                        act.wait_ge(s["ssq"], 2 * GT * (g + 1))
                        if g >= 1:
                            act.wait_ge(s["rkv"], g)
                        nc.scalar.activation(nrm[:, :, :], ssq[:, :, :], ACT.Sqrt).then_inc(s["norm"], 1)
                        for c in range(C):
                            act.wait_ge(s["q_ps"], C * g + c + 1)
                            if g >= 1:
                                act.wait_ge(s["o_ps"], GT * g)
                            nc.scalar.activation(qT[:, c, :], bank[5 + c][:, :], ACT.Identity,
                                                 bias=pwt("bq")[:, c:c + 1]).then_inc(s["qT"], 1)
                store_xn(front, NG - 1)

            act.wait_ge(pw_in, 48)
            ffn_front(ffn[0])
            tile_loop(ffn[0])
            attention(att, ffn[1])
            weights_exp(ffn[1])
            tile_loop(ffn[1])

        @block.tensor
        def _(pe):
            ident = const("ident")

            def group_transposes(s, g, b, xb):
                for c in range(C):
                    for t in range(GT):
                        mm = nc.tensor.transpose(bank[b + c][:, t * P:(t + 1) * P],
                                                 xn[:, xb, t, c * P:(c + 1) * P], ident)
                    mm.then_inc(s["xn_ps"], 1)

            def router(s, g, b, tb):
                pe.wait_ge(s["xnT"], C * (g + 1))
                for t in range(GT):
                    for c in range(C):
                        mm = nc.tensor.matmul(bank[b][:, t * EXPERTS:(t + 1) * EXPERTS],
                                              xnT[:, tb, c, t * P:(t + 1) * P], rw[:, c, :],
                                              start=(c == 0), stop=(c == C - 1))
                mm.then_inc(s["logit_ps"], 1)

            def ffn_front(s):
                for g in range(NG):
                    pe.wait_ge(s["xn"], g + 1)
                    if g >= 2:
                        pe.wait_ge(s["xnT"], C * (g - 1))
                    group_transposes(s, g, C * (g % 2), g % XBUF)
                    if g >= 2:
                        pe.wait_ge(s["logit"], g - 1)
                    if g == NG - 1:
                        sum_partitions(0)
                    router(s, g, 4 + g % 2, g % 2)
                    for k in range(GRAMS * g // (NG - 1), GRAMS * (g + 1) // (NG - 1) if g < NG - 1 else 0):
                        gram(0, k)

            def gram(g, k):
                e, b = divmod(k, WE // P)
                if k == 0:
                    pe.wait_ge(w_loaded[g], 16 * WB)
                    if g == 1:
                        pe.wait_ge(w_scales, g)
                block = raw_places[g * WB + e].bitcast(BF16).rearrange("p (b n two) -> p b n two", n=P,
                                                                      two=2)[:, b, :, 1]
                mm = nc.tensor.matmul(sums_bank(g)[:, e * P:(e + 1) * P], block, block,
                                      start=(b == 0), stop=(b == WE // P - 1))
                if k == GRAMS - 1:
                    mm.then_inc(w_grams, 1)

            def sum_partitions(g):
                pe.wait_ge(w_diag, g + 1)
                pe.wait_ge(ones_set, 3)
                nc.tensor.matmul(sums_bank(g)[:, 0:WB], ones32, wsq[:, g * WB:(g + 1) * WB],
                                 start=True, stop=True).then_inc(w_sums, 1)

            def weights_norms(g):
                for k in range(GRAMS):
                    gram(g, k)
                sum_partitions(g)

            def routing(s, first):
                if first:
                    weights_norms(1)
                pe.wait_ge(s["pre"], 1)
                nc.tensor.matmul(bank[6][:, 0:EXPERTS * NT], onesb[:, :], pre, start=True, stop=False)
                nc.tensor.matmul(bank[6][:, 0:EXPERTS * NT], lowm, mask, start=False, stop=True)
                nc.tensor.matmul(bank[6][:, EXPERTS * NT:EXPERTS * NT + EXPERTS], onesb[:, :],
                                 pre.rearrange("p (e i) -> p e i", e=EXPERTS)[:, :, NT - 1],
                                 start=True, stop=True).then_inc(s["cnt_ps"], 1)
                if first:
                    weights_norms(2)
                pe.wait_ge(s["ecol"], 1)
                nc.tensor.matmul(bank[6][0:1, 0:P], ecol, ident, start=True, stop=True).then_inc(s["etile_ps"], 1)
                for n in range(TOP_K * NT):
                    if first and GRAMS_AT <= n < SUMS_AT:
                        for k in range(4 * (n - GRAMS_AT), 4 * (n - GRAMS_AT) + 4):
                            gram(3, k)
                    if first and n == SUMS_AT:
                        sum_partitions(3)
                    pe.wait_ge(s["slot_hot"], n + 1)
                    if first:
                        pe.wait_ge(s["tile_hot"], n + 1)
                    elif n % 3 == 2:
                        pe.wait_ge(s["tile_hot_pool"], n // 3 + 1)
                    else:
                        pe.wait_ge(s["tile_hot"], n - n // 3 + 1)
                    k, i = divmod(n, NT)
                    nc.tensor.matmul(bank[7][:, k * TILES:(k + 1) * TILES], slot_hot[:, n % RING, :],
                                     tile_hot[:, n % RING, :], start=(i == 0),
                                     stop=(i == NT - 1)).then_inc(s["place_ps"], 1)

            def turn_x(s, j, u, lo):
                pe.wait_ge(s["gathered"][u], 4 * j - 4 * u + 16)
                if lo >= 2:
                    pe.wait_ge(s["xt"], j - 1)
                for c in range(2 * C):
                    mm = nc.tensor.transpose(turned(u % 2)[:, c * P:(c + 1) * P], xg[:, u, c * P:(c + 1) * P], ident16)
                mm.then_inc(s["xt_ps"], 1)

            def expert(w, e, at, n):
                return w16[:, bass.ds(e, 1), w * WE + at:w * WE + at + n].rearrange("p o n -> p (o n)")

            PARTS = ((0, 0), (0, 1), (1, 0))

            def bias_product(acc, e, at, w):
                nc.tensor.matmul(acc, pick[:, bass.ds(e, 1)].to_broadcast([P, P]), biases[:, at:at + w],
                                 start=True, stop=False)

            def gate_up(s, j, b, lo, e):
                if lo >= 2:
                    pe.wait_ge(s["up"], j - 1)
                acc = bank[2 + b][:, :]
                bias_product(acc, e, 0, GU)
                pe.wait_ge(s["xt"], j + 1)
                for c in range(C):
                    for x, w in PARTS:
                        mm = nc.tensor.matmul(acc, xT[:, b, x, c, :], expert(w, e, c * GU, GU),
                                              start=False, stop=(c == C - 1 and (x, w) == PARTS[-1]))
                mm.then_inc(s["gu_ps"], 1)

            def turn_h(s, j, b, lo):
                pe.wait_ge(s["hid"], j + 1)
                if lo >= 2:
                    pe.wait_ge(s["hid_lo"], j - 1)
                for c in range(C):
                    mm = nc.tensor.transpose(bank[4 + b][:, c * P:(c + 1) * P], hid[:, b, c * P:(c + 1) * P], ident)
                mm.then_inc(s["ht_ps"], 1)

            def down(s, j, b, lo, e):
                if lo >= 2:
                    pe.wait_ge(s["y"], j - 1)
                acc = bank[6 + b][:, 0:D]
                bias_product(acc, e, GU, D)
                pe.wait_ge(s["hid_lo"], j + 1)
                for c in range(C):
                    for h, w in PARTS:
                        mm = nc.tensor.matmul(acc, hT[:, b, h, c, :], expert(w, e, C * GU + c * D, D),
                                              start=False, stop=(c == C - 1 and (h, w) == PARTS[-1]))
                mm.then_inc(s["y_ps"], 1)

            def tile(s, j, u, nxt, prv, prv2, lo, e, e2):
                if nxt:
                    turn_x(s, j + 1, (u + 1) % UNROLL, lo + 1)
                gate_up(s, j, u % 2, lo, e)
                if prv:
                    turn_h(s, j - 1, (u + 1) % 2, lo - 1)
                if prv2:
                    down(s, j - 2, u % 2, lo - 2, e2)

            def experts_of(j, count):
                return experts_into_registers(etile[0:1, bass.ds(j, count)], mybir.EngineType.PE)

            def tile_loop(s, first):
                pe.wait_ge(s["etile"], 1)
                if first:
                    pe.wait_ge(w_lo, POOL_ALL)
                    pe.wait_ge(w_lo_dve, NG - 1)
                    pe.wait_ge(table_set, 1)
                    pe.wait_ge(bias_rows, 32)
                turn_x(s, 0, 0, 0)
                e = experts_of(0, LONG)
                for u in range(LONG):
                    tile(s, u, u, True, u >= 1, u >= 2, u, e[u], e[u - 2] if u >= 2 else None)
                with pe.Fori(LONG, TILES - 2 * LONG + 1, LONG) as j0:
                    e = experts_of(j0 - 2, LONG + 2)
                    for u in range(LONG):
                        tile(s, j0 + u, u, True, True, True, LONG, e[u + 2], e[u])
                e = experts_of(TILES - LONG - 2, LONG + 2)
                for u in range(LONG):
                    j = TILES - LONG + u
                    tile(s, j, u, u < LONG - 1, True, True, j, e[u + 2], e[u])
                turn_h(s, TILES - 1, 1, TILES - 1)
                down(s, TILES - 2, 0, TILES - 2, e[LONG])
                down(s, TILES - 1, 1, TILES - 1, e[LONG + 1])

            def mix(s, g):
                pe.wait_ge(s["rkv"], g + 1)
                pe.wait_ge(s["kvprod"], GT * (g + 1))
                pe.wait_ge(s["kvpass"], GT * (g + 1))
                for b in range(2):
                    for c in range(C):
                        for h in range(2):
                            t = 2 * b + h
                            mm = nc.tensor.matmul(bank[4][:, 2 * b + c:2 * b + c + 1],
                                                  kvprod[:, t, c * P:(c + 1) * P], rkv[:, t:t + 1],
                                                  start=(h == 0), stop=(h == 1))
                mm.then_inc(s["a_ps"], 1)

            def project(s, g, tiles):
                for t in tiles:
                    n = g * GT + t
                    if t % 2 == 0:
                        pe.wait_ge(s["aw"], 2 * g + t // 2 + 1)
                    if t == 0:
                        pe.wait_ge(s["qT"], C * (g + 1))
                    if t == 0 and g >= 1:
                        pe.wait_ge(s["x2"], n)
                    elif t == GT - 1:
                        pe.wait_ge(s["x2"], n - GT + 2)
                    acc = bank[OUT_BANKS[t]][:, 0:D]
                    nc.tensor.matmul(acc, pick[:, EXPERTS + 1:EXPERTS + 2].to_broadcast([P, P]), bout,
                                     start=True, stop=False)
                    for c in range(C):
                        mm = nc.tensor.matmul(acc, qT[:, c, t * P:(t + 1) * P], aw[:, t // 2, c, :],
                                              start=False, stop=(c == C - 1))
                    mm.then_inc(s["o_ps"], 1)

            def keys_values(s, g):
                pe.wait_ge(s["xnT"], C * (g + 1))
                for t in range(GT):
                    n = g * GT + t
                    if n >= 2:
                        pe.wait_ge(s["kv"], n - 1)
                        pe.wait_ge(s["ssq"], 2 * (n - 1))
                    nc.tensor.matmul(bank[2 + n % 2][:, :], pick[:, EXPERTS:EXPERTS + 1].to_broadcast([P, P]), bkv,
                                     start=True, stop=False)
                    for c in range(C):
                        mm = nc.tensor.matmul(bank[2 + n % 2][:, :], xnT[:, 0, c, t * P:(t + 1) * P],
                                              win[:, c, D:3 * D], start=False, stop=(c == C - 1))
                    mm.then_inc(s["kv_ps"], 1)

            def queries(s, g):
                if g >= 1:
                    pe.wait_ge(s["x2"], GT * g)
                for m in range(C):
                    if g >= 1:
                        pe.wait_ge(s["qT"], C * (g - 1) + m + 1)
                    for c in range(C):
                        mm = nc.tensor.matmul(bank[5 + m][:, :], win[:, c, m * P:(m + 1) * P], xnT[:, 0, c, :],
                                              start=(c == 0), stop=(c == C - 1))
                    mm.then_inc(s["q_ps"], 1)

            def attention(s, front):
                for g in range(NG + 1):
                    if g >= 1:
                        if g >= 2:
                            pe.wait_ge(front["logit"], g - 1)
                        mix(s, g - 1)
                        project(s, g - 1, range(GT // 2))
                    if g < NG:
                        pe.wait_ge(s["xn"], g + 1)
                        if g >= 2:
                            pe.wait_ge(front["xnT"], C * (g - 1))
                        elif g == 1:
                            pe.wait_ge(s["xnT"], C)
                        group_transposes(s, g, 0, 1)
                    if g >= 1:
                        project(s, g - 1, range(GT // 2, GT))
                    if g < NG:
                        keys_values(s, g)
                    if g >= 1:
                        pe.wait_ge(front["xn"], g)
                        pe.wait_ge(s["xnT"], C * min(g + 1, NG))
                        if g == NG:
                            pe.wait_ge(front["xnT"], C * (g - 1))
                        group_transposes(front, g - 1, 0, 2)
                    if g < NG:
                        queries(s, g)
                    if g >= 1:
                        pe.wait_ge(s["amix"], g)
                        router(front, g - 1, 4, 1)

            pe.wait_ge(const_in, 32)
            pe.wait_ge(pw_in, 48)
            ffn_front(ffn[0])
            routing(ffn[0], True)
            tile_loop(ffn[0], True)
            pe.wait_ge(attw_in, 32)
            attention(att, ffn[1])
            routing(ffn[1], False)
            tile_loop(ffn[1], False)

        @block.vector
        def _(dve):
            done = [0]
            V = nc.vector

            def step(ins):
                done[0] += 1
                ins.then_inc(dve_step, 1)
                return done[0]

            def settled(n=None):
                dve.wait_ge(dve_step, done[0] if n is None else n)

            def aggregate(s, b):
                settled()
                for t in range(GT):
                    m = V.bn_aggr(mv[:, b, t, :], stats[:, b, t, :])
                    if t < GT - 1:
                        step(m)
                    else:
                        m.then_inc(s["var"], 1)

            def normalise(s, b, count, src, dst, signal):
                dve.wait_ge(s["std"], count)
                step(V.reciprocal(rstd[:, b, :], rstd[:, b, :]))
                dve.wait_ge(s["var"], count)
                settled()
                apply(b, src, dst, signal)

            def apply(b, src, dst, signal):
                for t in range(GT):
                    m = V.tensor_scalar(dst(t), src(t), mv[:, b, t, 0:1], rstd[:, b, t:t + 1],
                                        ALU.subtract, ALU.mult)
                    if t == GT - 1:
                        m.then_inc(signal, 1)
                    else:
                        step(m)

            def top4(s, g, b):
                dve.wait_ge(s["logit_ps"], g + 1)
                V.tensor_tensor(logits[:, g * GT:(g + 1) * GT, :],
                                bank[b][:, 0:GT * EXPERTS].rearrange("p (t e) -> p t e", e=EXPERTS),
                                rb[:, :].unsqueeze(1).to_broadcast([P, GT, EXPERTS]),
                                ALU.add).then_inc(s["logit"], 1)
                dve.wait_ge(s["logit"], g + 1)
                for t in range(g * GT, (g + 1) * GT):
                    step(V.max(tops[:, t, :], logits[:, t, :]))
                settled()
                for t in range(g * GT, (g + 1) * GT):
                    step(V.max_index(topi[:, t, :], tops[:, t, :], logits[:, t, :]))

            def ffn_front(s):
                def stats_of(g):
                    dve.wait_ge(x_in[g], 16)
                    for t in range(GT):
                        step(V.bn_stats(stats[:, g % 2, t, :], X[:, g * GT + t, :]))
                    aggregate(s, g % 2)

                stats_of(0)
                for g in range(NG):
                    if g + 1 < NG:
                        stats_of(g + 1)
                    if g >= XBUF:
                        dve.wait_ge(s["xlo"], g - XBUF + 1)
                        dve.wait_ge(s["xn_ps"], C * (g - XBUF + 1))
                    normalise(s, g % 2, g + 1, lambda t: X[:, g * GT + t, :], lambda t: xn[:, g % XBUF, t, :],
                              s["xn"])
                    if g >= 1:
                        top4(s, g - 1, 4 + (g - 1) % 2)
                scales(0)
                top4(s, NG - 1, 4 + (NG - 1) % 2)

            def scales(g):
                a, b = g * WB, (g + 1) * WB
                dve.wait_ge(w_grams, g + 1)
                if g >= 1:
                    settled()
                step(V.tensor_tensor(wdiag[:, :, :], sums_bank(g)[:, :].rearrange("p (e n) -> p e n", e=WB),
                                     const("ident").unsqueeze(1).to_broadcast([P, WB, P]), ALU.mult))
                settled()
                V.tensor_reduce(wsq[:, a:b], wdiag[:, :, :], AX_X, ALU.add).then_inc(w_diag, 1)
                dve.wait_ge(w_sums, g + 1)
                step(V.tensor_copy(wtot[:, a:b], sums_bank(g)[:, 0:WB]))
                settled()
                step(V.tensor_scalar(wint[:, 0, a:b], wtot[:, a:b].bitcast(I32), 23, None, ALU.logical_shift_right))
                settled()
                step(V.tensor_scalar(wint[:, 1, a:b], wint[:, 0, a:b], 1.0, None, ALU.add))
                settled()
                step(V.tensor_scalar(wint[:, 2, a:b], wint[:, 1, a:b], 1, None, ALU.logical_shift_right))
                settled()
                step(V.tensor_scalar(wint[:, 0, a:b], wint[:, 2, a:b], 38.0, -1.0, ALU.max, ALU.mult))
                step(V.tensor_scalar(wint[:, 1, a:b], wint[:, 2, a:b], 38.0, 49.0, ALU.max, ALU.add))
                settled()
                step(V.tensor_scalar(wint[:, 2, a:b], wint[:, 0, a:b], 205.0, None, ALU.add))
                step(V.tensor_scalar(winv[:, a:b].bitcast(I32), wint[:, 1, a:b], 23, None, ALU.logical_shift_left))
                settled()
                V.tensor_scalar(wscale[:, a:b].bitcast(I32), wint[:, 2, a:b], 23, None,
                                ALU.logical_shift_left).then_inc(w_scales, 1)

            def weights_lo(g):
                e = (g + 1) * WB - 1
                dve.wait_ge(w_hi, e + 1)
                V.scalar_tensor_tensor(w16[:, e, WE:2 * WE], raw_places[e], wscale[:, e:e + 1], w16[:, e, 0:WE],
                                       ALU.mult, ALU.subtract).then_inc(w_lo_dve, 1)

            def make_table():
                dve.wait_ge(w_scales, NG)
                settled()
                for k, src, factor in ((T_LIM, wscale, LIMIT), (T_NLIM, wscale, -LIMIT), (T_S, wscale, 1.0),
                                       (T_ALPHA, winv, ALPHA), (T_Y, winv, 1 / H_SCALE)):
                    step(V.tensor_scalar(table[:, :, k], src[:, :], factor, None, ALU.mult))
                step(V.scalar_tensor_tensor(table[:, :, T_HID], winv[:, :], H_SCALE, winv[:, :], ALU.mult,
                                            ALU.mult))
                for at, factor in ((EXPERTS, 1.0), (EXPERTS + 1, 1 / H_SCALE)):
                    step(V.tensor_scalar(pick[:, at:at + 1], const("emask")[:, EXPERTS:EXPERTS + 1], factor, None,
                                         ALU.mult))
                V.tensor_tensor(pick[:, 0:EXPERTS], const("emask")[:, 0:EXPERTS], wscale[:, :],
                                ALU.mult).then_inc(table_set, 1)

            def split_biases():
                outputs = bsrc[:, BCOL * GU // BW:BCOL]
                step(V.tensor_scalar(outputs, outputs, H_SCALE, None, ALU.mult))
                settled()
                step(V.tensor_copy(bpart[:, 0, :], bsrc))
                settled()
                step(V.tensor_tensor(bres, bsrc, bpart[:, 0, :], ALU.subtract))
                settled()
                step(V.tensor_copy(bpart[:, 1, :], bres))
                settled()
                step(V.tensor_tensor(bres2, bres, bpart[:, 1, :], ALU.subtract))
                settled()
                V.tensor_copy(bpart[:, 2, :], bres2).then_inc(bias_split, 1)

            def routing(s, first):
                settled()
                step(V.tensor_copy(topif[:, :, :], topi[:, :, 0:TOP_K]))
                V.tensor_tensor(wk[:, :, :], tops[:, :, 0:TOP_K],
                                tops[:, :, 0:1].to_broadcast([P, NT, TOP_K]), ALU.subtract).then_inc(s["wexp_in"], 1)
                settled()
                step(V.tensor_tensor(hot[:, :, :, :],
                                     const("iota").unsqueeze(1).unsqueeze(3)
                                     .to_broadcast([P, TOP_K, EXPERTS, NT]),
                                     topif.rearrange("p i k -> p k i").unsqueeze(2)
                                     .to_broadcast([P, TOP_K, EXPERTS, NT]), ALU.is_equal))
                settled()
                flat = hot.rearrange("p k e i -> p k (e i)")
                step(V.tensor_tensor(hot2, flat[:, 0:2, :], flat[:, 2:4, :], ALU.add))
                settled()
                step(V.tensor_tensor(mask, hot2[:, 0, :], hot2[:, 1, :], ALU.add))
                settled()
                V.tensor_tensor_scan(pre, const("seg"), mask, 0.0, ALU.mult, ALU.add).then_inc(s["pre"], 1)
                if first:
                    scales(1)
                    weights_lo(0)
                dve.wait_ge(s["cnt_ps"], 1)
                step(V.tensor_scalar(cnti, bank[6][:, EXPERTS * NT:EXPERTS * NT + EXPERTS], float(P - 1),
                                     None, ALU.add))
                settled()
                step(V.tensor_scalar(nt128, cnti, 7, 7, ALU.logical_shift_right, ALU.logical_shift_left))
                settled()
                step(V.tensor_tensor_scan(tend, onesb[:, 0:EXPERTS], nt128, 0.0, ALU.mult, ALU.add))
                settled()
                step(V.tensor_tensor(base, tend, nt128, ALU.subtract))
                settled()
                step(V.tensor_tensor(posall[:, :, :],
                                     bank[6][:, 0:EXPERTS * NT].rearrange("p (e i) -> p e i", e=EXPERTS),
                                     base.unsqueeze(2).to_broadcast([P, EXPERTS, NT]), ALU.add))
                settled()
                step(V.tensor_tensor(hotpos.rearrange("p k e i -> p k (e i)"), flat,
                                     posall.rearrange("p e i -> p (e i)").unsqueeze(1)
                                     .to_broadcast([P, TOP_K, EXPERTS * NT]), ALU.mult))
                step(V.tensor_scalar(ecmp, tend, const("part128"), None, ALU.is_le))
                settled()
                step(V.tensor_reduce(pos.rearrange("p (k i) -> p k i", k=TOP_K),
                                     hotpos.rearrange("p k e i -> p k i e"), AX_X, ALU.add))
                step(V.tensor_reduce(ecol, ecmp, AX_X, ALU.add))
                settled()
                step(V.tensor_copy(posi, pos))
                V.tensor_scalar(ecol, ecol, float(EXPERTS - 1), None, ALU.min).then_inc(s["ecol"], 1)
                settled()
                step(V.tensor_scalar(ji, posi, 7, None, ALU.logical_shift_right))
                settled()
                V.tensor_copy(jf, ji).then_inc(s["hot"], 1)
                dve.wait_ge(s["hot"], 1)
                step(V.scalar_tensor_tensor(sf, jf, -float(P), pos, ALU.mult, ALU.add))
                settled()
                for n in range(TOP_K * NT):
                    if first and n == BATCH2_AT:
                        scales(2)
                        weights_lo(1)
                    if first and n == SUMS_AT:
                        scales(3)
                        make_table()
                    if first and n == LO_AT:
                        weights_lo(2)
                    if n >= RING:
                        dve.wait_ge(s["place_ps"], n - RING + 1)
                    if first or n % 3 != 2:
                        V.tensor_scalar(tile_hot[:, n % RING, :], iota16[:, 0:TILES], jf[:, n:n + 1],
                                        const("tid1")[:, n % NT:n % NT + 1], ALU.is_equal,
                                        ALU.mult).then_inc(s["tile_hot"], 1)
                    V.tensor_scalar(slot_hot[:, n % RING, :], iota16, sf[:, n:n + 1], None,
                                    ALU.is_equal).then_inc(s["slot_hot"], 1)
                dve.wait_ge(s["wexp"], 1)
                step(V.tensor_reduce(wsum, wk[:, :, :], AX_X, ALU.add))
                settled()
                step(V.reciprocal(wrec, wsum))
                settled()
                step(V.scalar_tensor_tensor(wk[:, :, :], wk[:, :, :], 0.5,
                                            wrec.unsqueeze(2).to_broadcast([P, NT, TOP_K]), ALU.mult, ALU.mult))
                dve.wait_ge(s["etile_ps"], 1)
                V.tensor_copy(etile[0:1, :], bank[6][0:1, 0:P]).then_inc(s["etile"], 1)
                dve.wait_ge(s["place_ps"], TOP_K * NT)
                step(V.tensor_copy(codes[:, :, :], bank[7][:, 0:TOP_K * TILES].rearrange("p (k j) -> p k j", k=TOP_K)))
                settled()
                step(V.tensor_reduce(csum, codes.rearrange("p k j -> p j k"), AX_X, ALU.add))
                settled()
                V.tensor_scalar(gidx[:, :], csum, -1.0, 0.0, ALU.add, ALU.max).then_inc(s["gidx"], 1)
                step(V.tensor_scalar(ksum, codes[:, 1, :], 0.0, float(TOKENS), ALU.is_gt, ALU.mult))
                step(V.scalar_tensor_tensor(ppres, csum, 0.0, const("spare1"), ALU.is_equal, ALU.mult))
                for k in (2, 3):
                    step(V.tensor_scalar(codes[:, k, :], codes[:, k, :], 0.0, float(k * TOKENS), ALU.is_gt, ALU.mult))
                settled()
                step(V.tensor_tensor(ksum, ksum, codes[:, 2, :], ALU.add))
                step(V.tensor_tensor(ppres, ppres, csum, ALU.add))
                settled()
                step(V.tensor_tensor(ksum, ksum, codes[:, 3, :], ALU.add))
                settled()
                V.scalar_tensor_tensor(sidx[:, :], ksum, -1.0, ppres, ALU.add, ALU.add).then_inc(s["sidx"], 1)

            def tile(s, j, u, lo):
                b = u % 2
                gu = bank[2 + b]

                def col(k):
                    return cols[:, u % UNROLL, k:k + 1]

                dve.wait_ge(s["tcols"], j + 1)
                dve.wait_ge(s["gu_ps"], j + 1)
                if lo >= 2:
                    dve.wait_ge(s["sig"], j - 1)
                V.tensor_scalar(gate[:, b], gu[:, 0:HID], col(T_LIM), None, ALU.min).then_inc(s["gate"], 1)
                V.tensor_scalar(up[:, b], gu[:, HID:GU], col(T_LIM), col(T_NLIM), ALU.min, ALU.max).then_inc(s["up"], 1)
                if lo >= 1:
                    hidden_lo(s, j - 1, (u + 1) % 2)
                dve.wait_ge(s["gate"], j + 1)
                dve.wait_ge(s["up"], j + 1)
                V.scalar_tensor_tensor(prod[:, b], up[:, b], col(T_S), gate[:, b], ALU.add,
                                       ALU.mult).then_inc(s["prod"], 1)
                dve.wait_ge(s["prod"], j + 1)
                dve.wait_ge(s["sig"], j + 1)
                if lo >= 2:
                    dve.wait_ge(s["ht_ps"], j - 1)
                V.scalar_tensor_tensor(hid[:, b], prod[:, b], col(T_HID), sig[:, b], ALU.mult,
                                       ALU.mult).then_inc(s["hid"], 1)

            def hidden_lo(s, j, b):
                dve.wait_ge(s["hid_hi"], j + 1)
                V.tensor_tensor(hT[:, b, 1].rearrange("p c n -> p (c n)"), bank[4 + b][:, 0:D],
                                hT[:, b, 0].rearrange("p c n -> p (c n)"), ALU.subtract).then_inc(s["hid_lo"], 1)

            def tile_loop(s):
                for u in range(LONG):
                    tile(s, u, u, u)
                with dve.Fori(LONG, TILES - LONG + 1, LONG) as j0:
                    for u in range(LONG):
                        tile(s, j0 + u, u, LONG)
                hidden_lo(s, TILES - 1, 1)

            def combine(s, i, k, after, ring, buf):
                if k == 0:
                    dve.wait_ge(s["y_back"][i % ring], 16 * (i // ring + 1))
                else:
                    settled(after)
                m = V.scalar_tensor_tensor(X[:, i, :], buf[:, i % ring, k, :], wk[:, i, k:k + 1], X[:, i, :],
                                           ALU.mult, ALU.add)
                if k < TOP_K - 1:
                    return step(m)
                m.then_inc(s["combined"], 1)

            def combine_and_rotate(s, before, g, t):
                i, n = g * GT + t, (g - 1) * GT + t
                after = combine(before, i, 0, None, YC, yc) if g < NG else None
                if g >= 1:
                    dve.wait_ge(s["kv"], n + 1)
                    if n >= 1:
                        dve.wait_ge(s["kvprod"], n)
                    half = t % 2
                    cos = const("cos")[:, half * ROT:(half + 1) * ROT].unsqueeze(1).to_broadcast([P, 2, ROT])
                    k_and_v = kv[:, t, :].rearrange("p (m d) -> p m d", m=2)
                    at_rot = step(V.tensor_tensor(rot, k_and_v[:, :, 0:ROT], cos, ALU.mult))
                if g < NG:
                    after = combine(before, i, 1, after, YC, yc)
                if g >= 1:
                    sines = rots[:, n % 2, :].rearrange("p (m d) -> p m d", m=2)
                    dve.wait_ge(s["rots"], n + 1)
                    settled(at_rot)
                    step(V.tensor_tensor(rot[:, :, 0:HALF], rot[:, :, 0:HALF], sines[:, :, HALF:ROT], ALU.add))
                    at_rot = step(V.tensor_tensor(rot[:, :, HALF:ROT], rot[:, :, HALF:ROT], sines[:, :, 0:HALF],
                                                  ALU.add))
                if g < NG:
                    after = combine(before, i, 2, after, YC, yc)
                if g >= 1:
                    settled(at_rot)
                    if t == 0 and g >= 2:
                        dve.wait_ge(s["a_ps"], g - 1)
                    V.tensor_tensor(kvprod[:, t, 0:ROT], rot[:, 0, :], rot[:, 1, :],
                                    ALU.mult).then_inc(s["kvprod"], 1)
                if g < NG:
                    combine(before, i, 3, after, YC, yc)
                    dve.wait_ge(before["combined"], i + 1)
                    step(V.bn_stats(stats[:, 0, t, :], X[:, i, :]))

            def attention(s, before, front):
                step(V.memset(mv[:, 1, :, 0], 0.0))
                for g in range(NG + 1):
                    for t in range(GT):
                        combine_and_rotate(s, before, g, t)
                    if g >= 2:
                        top4(front, g - 2, 4)
                    if g < NG:
                        aggregate(s, 0)
                    if g >= 1:
                        dve.wait_ge(s["norm"], g)
                        if g >= 2:
                            dve.wait_ge(s["a_ps"], g - 1)
                        step(V.tensor_tensor(rkv[:, :], nrm[:, :, 0], nrm[:, :, 1], ALU.mult))
                        settled()
                        V.reciprocal(rkv[:, :], rkv[:, :]).then_inc(s["rkv"], 1)
                    if g < NG:
                        dve.wait_ge(s["std"], 2 * g + 1)
                        step(V.reciprocal(rstd[:, 0, :], rstd[:, 0, :]))
                        dve.wait_ge(s["var"], 2 * g + 1)
                        settled()
                        step(V.tensor_tensor(mv[:, 1, :, 1], mv[:, 0, :, 1], rstd[:, 0, :], ALU.mult))
                        settled()
                        V.tensor_tensor(mv[:, 1, :, 1], mv[:, 1, :, 1], rstd[:, 0, :], ALU.mult).then_inc(s["var"], 1)
                        if g >= 1:
                            dve.wait_ge(s["xsum"], GT * g)
                        apply(0, lambda t: X[:, g * GT + t, :], lambda t: xn[:, 0, t, :], s["xin"])
                        dve.wait_ge(s["xin"], g + 1)
                    if g >= 1:
                        dve.wait_ge(s["a_ps"], g)
                        V.tensor_scalar(amix.rearrange("p b c -> p (b c)"), bank[4][:, 0:2 * C], 0.5, 0.5, ALU.mult,
                                        ALU.add).then_inc(s["amix"], 1)
                    if g < NG:
                        if g >= 1:
                            dve.wait_ge(s["xn_ps"], C * g)
                        normalise(s, 1, 2 * g + 2, lambda t: xn[:, 0, t, :], lambda t: xn[:, 1, t, :], s["xn"])
                    if g >= 1:
                        dve.wait_ge(s["xsum"], GT * g)
                        for t in range(GT):
                            n = (g - 1) * GT + t
                            dve.wait_ge(s["o_ps"], n + 1)
                            V.tensor_tensor(X[:, n, :], bank[OUT_BANKS[t]][:, 0:D], X[:, n, :],
                                            ALU.add).then_inc(s["x2"], 1)
                            dve.wait_ge(s["x2"], n + 1)
                            step(V.bn_stats(stats[:, 2, t, :], X[:, n, :]))
                        aggregate(front, 2)
                        if g >= 2:
                            dve.wait_ge(front["xlo"], g - 1)
                            dve.wait_ge(front["xn_ps"], C * (g - 1))
                        normalise(front, 2, g, lambda t: X[:, (g - 1) * GT + t, :], lambda t: xn[:, 2, t, :],
                                  front["xn"])
                top4(front, NG - 1, 4)

            dve.wait_ge(const_in, 32)
            dve.wait_ge(pw_in, 48)
            split_biases()
            dve.wait_ge(ones_set, 3)
            ffn_front(ffn[0])
            routing(ffn[0], True)
            tile_loop(ffn[0])
            dve.wait_ge(attw_in, 32)
            attention(att, ffn[0], ffn[1])
            routing(ffn[1], False)
            tile_loop(ffn[1])
            for i in range(0, NT, 2):
                after = [None, None]
                for k in range(TOP_K):
                    for h in range(2):
                        after[h] = combine(ffn[1], i + h, k, after[h], YL, yl)


def _constants():
    p = np.arange(P)
    c = np.zeros((P, CONST_W), np.float32)

    def put(name, v):
        at, w = CONST[name]
        c[:, at:at + w] = np.asarray(v, np.float32).reshape(-1, w) if np.ndim(v) else v

    put("ident", np.eye(P))
    put("iota", np.tile(np.arange(EXPERTS), (P, 1)))
    put("seg", np.tile((np.arange(EXPERTS * NT) % NT != 0), (P, 1)))
    put("tid1", np.arange(NT)[None, :] * P + p[:, None] + 1)
    put("part128", p[:, None] * P)
    put("emask", (p[:, None] % (EXPERTS + 1) == np.arange(EXPERTS + 1)[None, :]) & (p[:, None] < BROWS))
    put("spare1", TOP_K * TOKENS + np.arange(TILES)[None, :] * P + p[:, None] + 1)
    inv = (1.0 / 10000.0 ** (np.arange(0, ROT, 2, dtype=np.float32) / np.float32(ROT))).astype(np.float32)
    ang = (np.arange(SEQ, dtype=np.float32)[:, None] * inv[None, :]).astype(np.float32)
    cos, sin = np.cos(ang), np.sin(ang)
    put("cos", np.concatenate([np.concatenate([cos[h * P:(h + 1) * P]] * 2, 1) for h in range(2)], 1))
    put("sin", np.concatenate([np.concatenate([sin[h * P:(h + 1) * P], -sin[h * P:(h + 1) * P]], 1) for h in range(2)], 1))
    c16 = np.concatenate([(p[:, None] < p[None, :]) - 1.0, np.tile(p, (P, 1)), np.eye(P)], 1).astype(np.float16)
    return c, c16


def kernel(**inputs):
    import concourse.bacc as _bacc
    from concourse.bass_utils import run_bass_kernel_spmd as _run

    a = {k[3:]: np.asarray(v) for k, v in inputs.items()}
    perm = np.concatenate([np.arange(0, ROT, 2), np.arange(1, ROT, 2), np.arange(ROT, D)])
    perm3 = np.concatenate([perm, D + perm, 2 * D + perm])

    def chunks(w):
        return w.reshape(C, P, -1).transpose(1, 0, 2)

    w_in = chunks(a["attn_W_in"][:, perm3])
    w_out = chunks(a["attn_W_out"][perm, :])
    b_in = a["attn_b_in"][perm3]
    w_gu = a["ffn_gate_up_proj"].reshape(EXPERTS, C, P, HID, 2).transpose(2, 0, 1, 4, 3).reshape(P, EXPERTS, C * GU)
    w_dn = a["ffn_down_proj"].reshape(EXPERTS, C, P, D).transpose(2, 0, 1, 3).reshape(P, EXPERTS, C * D)
    b_gu = a["ffn_gate_up_proj_bias"].reshape(EXPERTS, HID, 2).transpose(0, 2, 1).reshape(EXPERTS, GU)
    bias = np.concatenate([np.concatenate([b_gu.ravel(), b_in[D:]]).reshape(P, -1),
                           np.concatenate([a["ffn_down_proj_bias"].ravel(), a["attn_b_out"]]).reshape(P, -1)], 1)
    pweights = np.concatenate([
        chunks(a["ffn_router_weight"].T).reshape(P, -1), a["attn_gamma"].reshape(C, P).T,
        a["attn_beta"].reshape(C, P).T, b_in[:D].reshape(C, P).T], 1)
    consts, consts16 = _constants()
    sent = {"x": a["attn_X"].reshape(TOKENS, D), "consts": consts, "consts16": consts16, "rbias": a["ffn_router_bias"], "pweights": pweights,
            "w_in": w_in, "w_out": w_out, "w_exp": np.concatenate([w_gu, w_dn], 2), "bias": bias}
    nc = _bacc.Bacc("TRN2", target_bir_lowering=False, num_devices=1)
    arrays, args = {}, []
    for name, v in sent.items():
        v = np.ascontiguousarray(v)
        arrays[f"in_{name}"] = v
        args.append(nc.dram_tensor(f"in_{name}", v.shape, mybir.dt.from_np(v.dtype), kind="ExternalInput").ap())
    args.append(nc.dram_tensor("out", [TOKENS, D], F32, kind="ExternalOutput").ap())
    macaron_kernel(nc, *args)
    r = _run(nc, [arrays], core_ids=[0])
    return r.results[0]["out"].reshape(BATCH, SEQ, D)
```
